# Optimizing a Trainium2 kernel written in Bass

```python
import numpy as np
import jax
import jax.numpy as jnp

def _softmax(x, axis=-1):
    return jax.nn.softmax(x, axis=axis)

def _gelu(x):
    return jax.nn.gelu(x, approximate=True)

def _silu(x):
    return jax.nn.silu(x)

def _sigmoid(x):
    return jax.nn.sigmoid(x)

def _layernorm(x, axis=-1, eps=1e-05):
    m = jnp.mean(x, axis=axis, keepdims=True)
    v = jnp.var(x, axis=axis, keepdims=True)
    return (x - m) / jnp.sqrt(v + eps)

def _scatter_add(tgt, idx, src, axis=0):
    return tgt.at[idx].add(src)

def _segment_sum(src, seg, n):
    return jax.ops.segment_sum(src, seg, n)
kernel_name = 'mk_gnn_resnorm_d2_gnn_r8_6f41d5'

def setup_inputs(seed: int=0):
    np.random.seed(seed)
    _w = jnp.asarray

    def _rec_inputs():
        import jax
        import jax.numpy as jnp
        _gk = jax.random.key(seed)
        x = -0.000202 + 1 * jax.random.normal(jax.random.fold_in(_gk, 1), (12500, 128), jnp.float32)
        _s = jax.random.randint(jax.random.fold_in(_gk, 2), (100000,), 0, 12500, jnp.int32)
        _d = jax.random.randint(jax.random.fold_in(_gk, 3), (100000,), 0, 12500, jnp.int32)
        _loop = jnp.arange(12500, dtype=jnp.int32)
        src = jnp.concatenate([_s, _d, _loop])
        dst = jnp.concatenate([_d, _s, _loop])
        _o = jnp.argsort(dst, stable=True)
        src = src[_o]
        dst = dst[_o]
        edge_attr_128 = -5.16925e-05 + 1.00005 * jax.random.normal(jax.random.fold_in(_gk, 11), (212500, 128), jnp.float32)
        edge_type_8 = jax.random.randint(jax.random.fold_in(_gk, 13), (212500,), 0, 8, jnp.int32)
        return (x, src, dst, edge_attr_128, edge_type_8)
    x, src, dst, edge_attr_128, edge_type_8 = _rec_inputs()

    def _L0_gnn_setup():
        import jax, jax.numpy as jnp
        import numpy as np
        N_NODES = 6250
        N_EDGES = 80000
        N_REL = 8
        IN_C = 128
        OUT_C = 128
        key = jax.random.key(seed)
        k1, k2, k3, k4 = jax.random.split(key, 4)
        x = jax.random.normal(k1, (N_NODES, IN_C), dtype=jnp.float32)
        edge_index = jax.random.randint(k2, (2, N_EDGES), 0, N_NODES, dtype=jnp.int64)
        edge_type = jax.random.randint(k3, (N_EDGES,), 0, N_REL, dtype=jnp.int64)
        limit = float(np.sqrt(6.0 / (IN_C + OUT_C)))
        weight = jax.random.uniform(k4, (N_REL, IN_C, OUT_C), dtype=jnp.float32, minval=-limit, maxval=limit)
        bias = jnp.zeros((OUT_C,), dtype=jnp.float32)
        return {'x': x, 'edge_index': edge_index, 'edge_type': edge_type, 'weight': weight, 'bias': bias}
    _L0_gnn_all = _L0_gnn_setup()
    _L0_gnn_in = {k: v for k, v in _L0_gnn_all.items() if k in ('weight', 'bias')}
    del _L0_gnn_all

    def _L1_gnn_setup():
        import jax, jax.numpy as jnp
        import numpy as np
        EPS = 1e-05
        GROUPS = 8

        def group_norm(h, w, b):
            N, C = h.shape
            hr = h.reshape(N, GROUPS, C // GROUPS)
            mu = jnp.mean(hr, axis=-1, keepdims=True)
            var = jnp.mean((hr - mu) ** 2, axis=-1, keepdims=True)
            hn = ((hr - mu) * jax.lax.rsqrt(var + EPS)).reshape(N, C)
            return hn * w + b
        key = jax.random.key(seed)
        ks = jax.random.split(key, 16)
        N, E = (6250, 100000)
        d_node, d_edge = (128, 128)
        h1a, h1b, h2a, d_out = (256, 128, 256, 128)

        def lin(k, fan_in, fan_out):
            lim = 1.0 / np.sqrt(fan_in)
            kw, kb = jax.random.split(k)
            W = jax.random.uniform(kw, (fan_in, fan_out), minval=-lim, maxval=lim, dtype=jnp.float32)
            b = jax.random.uniform(kb, (fan_out,), minval=-lim, maxval=lim, dtype=jnp.float32)
            return (W, b)
        x = jax.random.normal(ks[0], (N, d_node), dtype=jnp.float32)
        edge_index = jax.random.randint(ks[1], (2, E), 0, N, dtype=jnp.int64)
        edge_attr = jax.random.normal(ks[2], (E, d_edge), dtype=jnp.float32)
        W1a, b1a = lin(ks[3], d_node + d_edge, h1a)
        W1b, b1b = lin(ks[4], h1a, h1b)
        W2a, b2a = lin(ks[5], d_node + h1b, h2a)
        W2b, b2b = lin(ks[6], h2a, d_out)
        return {'x': x, 'edge_index': edge_index, 'edge_attr': edge_attr, 'W1a': W1a, 'b1a': b1a, 'gn1a_w': jnp.ones((h1a,), jnp.float32), 'gn1a_b': jnp.zeros((h1a,), jnp.float32), 'W1b': W1b, 'b1b': b1b, 'gn1b_w': jnp.ones((h1b,), jnp.float32), 'gn1b_b': jnp.zeros((h1b,), jnp.float32), 'W2a': W2a, 'b2a': b2a, 'gn2a_w': jnp.ones((h2a,), jnp.float32), 'gn2a_b': jnp.zeros((h2a,), jnp.float32), 'W2b': W2b, 'b2b': b2b}
    _L1_gnn_all = _L1_gnn_setup()
    _L1_gnn_in = {k: v for k, v in _L1_gnn_all.items() if k in ('W1a', 'b1a', 'gn1a_w', 'gn1a_b', 'W1b', 'b1b', 'gn1b_w', 'gn1b_b', 'W2a', 'b2a', 'gn2a_w', 'gn2a_b', 'W2b', 'b2b')}
    del _L1_gnn_all
    return {'x': x, 'src': src, 'dst': dst, 'edge_attr_128': edge_attr_128, 'edge_type_8': edge_type_8, 'L0_gnn_weight': _L0_gnn_in['weight'], 'L0_gnn_bias': _L0_gnn_in['bias'], 'L1_gnn_W1a': _L1_gnn_in['W1a'], 'L1_gnn_b1a': _L1_gnn_in['b1a'], 'L1_gnn_gn1a_w': _L1_gnn_in['gn1a_w'], 'L1_gnn_gn1a_b': _L1_gnn_in['gn1a_b'], 'L1_gnn_W1b': _L1_gnn_in['W1b'], 'L1_gnn_b1b': _L1_gnn_in['b1b'], 'L1_gnn_gn1b_w': _L1_gnn_in['gn1b_w'], 'L1_gnn_gn1b_b': _L1_gnn_in['gn1b_b'], 'L1_gnn_W2a': _L1_gnn_in['W2a'], 'L1_gnn_b2a': _L1_gnn_in['b2a'], 'L1_gnn_gn2a_w': _L1_gnn_in['gn2a_w'], 'L1_gnn_gn2a_b': _L1_gnn_in['gn2a_b'], 'L1_gnn_W2b': _L1_gnn_in['W2b'], 'L1_gnn_b2b': _L1_gnn_in['b2b']}

def reference(x, src, dst, edge_attr_128, edge_type_8, L0_gnn_weight, L0_gnn_bias, L1_gnn_W1a, L1_gnn_b1a, L1_gnn_gn1a_w, L1_gnn_gn1a_b, L1_gnn_W1b, L1_gnn_b1b, L1_gnn_gn1b_w, L1_gnn_gn1b_b, L1_gnn_W2a, L1_gnn_b2a, L1_gnn_gn2a_w, L1_gnn_gn2a_b, L1_gnn_W2b, L1_gnn_b2b):
    import jax
    import jax.numpy as jnp

    def _L0_gnn_ref(x, edge_index, edge_type, weight, bias):
        import jax, jax.numpy as jnp
        import numpy as np
        N_NODES = 6250
        N_EDGES = 80000
        N_REL = 8
        IN_C = 128
        OUT_C = 128
        x_transformed = jnp.einsum('ni,rio->rno', x, weight)
        row = edge_index[0]
        col = edge_index[1]
        messages = x_transformed[edge_type, col]
        out = jax.ops.segment_sum(messages, row, num_segments=x.shape[0])
        return out + bias

    def _L1_gnn_ref(x, edge_index, edge_attr, W1a, b1a, gn1a_w, gn1a_b, W1b, b1b, gn1b_w, gn1b_b, W2a, b2a, gn2a_w, gn2a_b, W2b, b2b):
        import jax, jax.numpy as jnp
        import numpy as np
        EPS = 1e-05
        GROUPS = 8

        def group_norm(h, w, b):
            N, C = h.shape
            hr = h.reshape(N, GROUPS, C // GROUPS)
            mu = jnp.mean(hr, axis=-1, keepdims=True)
            var = jnp.mean((hr - mu) ** 2, axis=-1, keepdims=True)
            hn = ((hr - mu) * jax.lax.rsqrt(var + EPS)).reshape(N, C)
            return hn * w + b
        N = x.shape[0]
        row, col = (edge_index[0], edge_index[1])
        se = jnp.concatenate([x[row], edge_attr], axis=1)
        h = jax.nn.relu(group_norm(se @ W1a + b1a, gn1a_w, gn1a_b))
        h = jax.nn.relu(group_norm(h @ W1b + b1b, gn1b_w, gn1b_b))
        sums = jax.ops.segment_sum(h, col, num_segments=N)
        cnt = jax.ops.segment_sum(jnp.ones((h.shape[0],), h.dtype), col, num_segments=N)
        agg = sums / jnp.maximum(cnt, 1.0)[:, None]
        u = jnp.concatenate([x, agg], axis=1)
        g = jax.nn.relu(group_norm(u @ W2a + b2a, gn2a_w, gn2a_b))
        return g @ W2b + b2b
    edge_index = jnp.stack([src, dst])
    x = _layernorm(x + _L0_gnn_ref(x, edge_index, edge_type_8, L0_gnn_weight, L0_gnn_bias), axis=-1)
    x = _layernorm(x + _L1_gnn_ref(x, edge_index, edge_attr_128, L1_gnn_W1a, L1_gnn_b1a, L1_gnn_gn1a_w, L1_gnn_gn1a_b, L1_gnn_W1b, L1_gnn_b1b, L1_gnn_gn1b_w, L1_gnn_gn1b_b, L1_gnn_W2a, L1_gnn_b2a, L1_gnn_gn2a_w, L1_gnn_gn2a_b, L1_gnn_W2b, L1_gnn_b2b), axis=-1)
    return x

_drawn_inputs = setup_inputs


def setup_inputs(seed=0):
    import zlib

    import numpy as np

    out = dict(_drawn_inputs(seed))
    spreads = {'L0_gnn_bias': (0.0, 0.34),
     'L1_gnn_gn1a_w': (1.0, 0.6),
     'L1_gnn_gn1a_b': (0.0, 0.634),
     'L1_gnn_gn1b_w': (1.0, 0.2),
     'L1_gnn_gn1b_b': (0.0, 0.441),
     'L1_gnn_gn2a_w': (1.0, 0.2),
     'L1_gnn_gn2a_b': (0.0, 0.1)}
    factors = {'L1_gnn_b1a': 5.636, 'L1_gnn_b1b': 3.173}
    for name, (base, spread) in spreads.items():
        noise = np.random.default_rng([zlib.crc32(name.encode()), seed]).standard_normal(out[name].shape)
        drawn = base * np.exp(spread * noise) if base else spread * noise
        out[name] = jnp.asarray(drawn.astype(out[name].dtype))
    for name, factor in factors.items():
        out[name] = (out[name] * factor).astype(out[name].dtype)
    return out
```

```python
from contextlib import ExitStack

import numpy as np
import concourse.bass as bass
from concourse import mybir

FP32, BF16, I32 = mybir.dt.float32, mybir.dt.bfloat16, mybir.dt.int32
ALU, ACT, AX = mybir.AluOpType, mybir.ActivationFunctionType, mybir.AxisListType

P = 128
C = 128
R = 8
H = 256
G = 8
NODES, EDGES = 12500, 212500
EPS = 1e-5
NB = 7
BLOCKS = 14
BN = NB * P
N = BN * BLOCKS
QT = 4
QE = QT * P
T = 1664
Q = T // QT
TRASH = N
ROWS = N + P
KC = QT
SW = C + 1
RING = 2
BANK = 512


class Names:
    pass


def pipeline(eng, count, lag):
    head = lag + RING + (lag % 2)
    for s in range(head):
        yield s % RING, lambda L: s - L if 0 <= s - L < count else None
    with eng.Fori(head // RING, count // RING) as turn:
        for u in range(RING):
            yield u, lambda L: turn * RING + (u - L)
    for s in range(count, count + lag):
        yield s % RING, lambda L: s - L if 0 <= s - L < count else None


def had(q, n):
    return q - n >= 0 if isinstance(q, int) else True


def uses(q, slot, each):
    return (q - slot) * (each // RING) + each


def identity(nc, pool, eye, zeroed, made):
    nc.gpsimd.memset(eye, 0.0).then_inc(zeroed, 1)
    pool.wait_ge(zeroed, 1)
    nc.gpsimd.affine_select(out=eye, in_=eye, compare_op=ALU.not_equal, fill=1.0, base=0,
                            pattern=[[-1, P]], channel_multiplier=1).then_inc(made, 1)


def spread(per_group, parts, k):
    return per_group.unsqueeze(2).broadcast_to((parts, per_group.shape[1], k))


def phase_tables(nc, k):
    HALF = R * C // 2
    with ExitStack() as ctx:
        sb = lambda n, s, d: ctx.enter_context(nc.sbuf_tensor(n, s, d))
        sem = lambda n: ctx.enter_context(nc.semaphore(n))
        w = sb("t_w", [P, R * C], FP32)
        xT = sb("t_xT", [P, RING, P], FP32)
        y = sb("t_y", [P, RING, R * C], FP32)
        zeros = sb("t_zeros", [P, 1024], FP32)
        dst_i = sb("t_dst_i", [P, T], I32)
        trash = sb("t_trash", [P, 1], FP32)
        trash_i = sb("t_trash_i", [P, 1], I32)
        ps = ctx.enter_context(nc.psum_tensor("t_ps", [P, RING, R * C], FP32))
        w_in, keys_in, zeroed, zero_out = sem("t_w_in"), sem("t_keys_in"), sem("t_zeroed"), sem("t_zero_out")
        x_in = [sem(f"t_x_in{i}") for i in range(RING)]
        product, copied_a, copied_v = sem("t_product"), sem("t_copied_act"), sem("t_copied_dve")
        stored = [sem(f"t_stored{i}") for i in range(RING)]
        cast, keyed, ones, made, trash_made = sem("t_cast"), sem("t_keyed"), sem("t_ones"), sem("t_made"), sem("t_trash")
        tiles = N // P
        block = ctx.enter_context(nc.Block())

        @block.sync
        def _(sp):
            sp.dma_start(w[:], k.w_rel).then_inc(w_in, 16)
            sp.dma_start(k.src_idx[:], k.src_cols).then_inc(keys_in, 16)
            sp.dma_start(dst_i[:], k.dst_cols).then_inc(keys_in, 16)
            sp.dma_start(k.type_i[:], k.type_cols).then_inc(keys_in, 16)
            for slot, at in pipeline(sp, tiles, 2):
                if (t := at(0)) is not None:
                    if had(t, RING):
                        sp.wait_ge(product, t - 1)
                    sp.dma_start(xT[:, slot, :], k.x_T[:, bass.ds(t * P, P)]).then_inc(x_in[slot], 16)
                if (t := at(2)) is not None:
                    sp.wait_ge(copied_a, t + 1)
                    sp.wait_ge(copied_v, t + 1)
                    sp.dma_start(k.y[bass.ds(t * P, P), :], y[:, slot, :]).then_inc(stored[slot], 16)
            for slot in range(RING):
                sp.wait_ge(stored[slot], 16 * (tiles // RING))

        @block.tensor
        def _(pe):
            pe.wait_ge(w_in, 16)
            for slot, at in pipeline(pe, tiles, 0):
                t = at(0)
                pe.wait_ge(x_in[slot], uses(t, slot, 16))
                if had(t, RING):
                    pe.wait_ge(copied_a, t - 1)
                    pe.wait_ge(copied_v, t - 1)
                nc.tensor.matmul(ps[:, slot, 0:HALF], xT[:, slot, :], w[:, 0:HALF], start=True, stop=True)
                nc.tensor.matmul(ps[:, slot, HALF:2 * HALF], xT[:, slot, :], w[:, HALF:2 * HALF],
                                 start=True, stop=True).then_inc(product, 1)

        @block.scalar
        def _(act):
            for slot, at in pipeline(act, tiles, 0):
                t = at(0)
                act.wait_ge(product, t + 1)
                if had(t, RING):
                    act.wait_ge(stored[slot], uses(t - RING, slot, 16))
                nc.scalar.copy(y[:, slot, 0:HALF], ps[:, slot, 0:HALF]).then_inc(copied_a, 1)

        @block.vector
        def _(dve):
            nc.vector.memset(zeros[:], 0.0).then_inc(zeroed, 1)
            dve.wait_ge(keys_in, 48)
            dve.wait_ge(trash_made, 1)
            nc.vector.tensor_copy(k.src_f[:], k.src_idx[:]).then_inc(cast, 1)
            nc.vector.tensor_copy(k.dst_f[:], dst_i[:]).then_inc(cast, 1)
            nc.vector.tensor_copy(trash[:], trash_i[:]).then_inc(cast, 1)
            dve.wait_ge(cast, 3)
            nc.vector.tensor_scalar(k.src_trash[:], k.src_f[:], -1.0, trash[:], ALU.mult, ALU.add).then_inc(keyed, 1)
            nc.vector.tensor_scalar(k.dst_trash[:], k.dst_f[:], -1.0, trash[:], ALU.mult, ALU.add).then_inc(keyed, 1)
            for slot, at in pipeline(dve, tiles, 0):
                t = at(0)
                dve.wait_ge(product, t + 1)
                if had(t, RING):
                    dve.wait_ge(stored[slot], uses(t - RING, slot, 16))
                nc.vector.tensor_copy(y[:, slot, HALF:2 * HALF], ps[:, slot, HALF:2 * HALF]).then_inc(copied_v, 1)

        @block.gpsimd
        def _(pool):
            nc.gpsimd.iota(trash_i[:], pattern=[[0, 1]], base=TRASH, channel_multiplier=1).then_inc(trash_made, 1)
            nc.gpsimd.memset(k.lower[:], 1.0).then_inc(ones, 1)
            pool.wait_ge(ones, 1)
            nc.gpsimd.affine_select(out=k.lower[:], in_=k.lower[:], compare_op=ALU.is_gt, fill=0.0, base=0,
                                    pattern=[[-1, P]], channel_multiplier=1).then_inc(made, 1)
            pool.wait_ge(zeroed, 1)
            n = 0
            for table, width in ((k.sums0, C), (k.sums1, SW)):
                for c in range(KC):
                    per = ROWS * width // P
                    flat = table[c].rearrange("n w -> (n w)").rearrange("(p m) -> p m", p=P)
                    for a in range(0, per, 1024):
                        b = min(per, a + 1024)
                        nc.gpsimd.dma_start(flat[:, a:b], zeros[:, 0:b - a]).then_inc(zero_out, 16)
                        n += 1
            pool.wait_ge(zero_out, 16 * n)


def phase_weights(nc, k):
    with ExitStack() as ctx:
        sb = lambda n, s, d: ctx.enter_context(nc.sbuf_tensor(n, s, d))
        sem = lambda n: ctx.enter_context(nc.semaphore(n))
        mean = sb("w_mean", [P, G], FP32)
        rows = {"b1b": (k.b1b, C, True), "b2a": (k.b2a, H, True), "b2b": (k.b2b, C, False)}
        row = {n: sb(f"w_{n}", [1, w], FP32) for n, (_, w, _) in rows.items()}
        part = {n: sb(f"w_{n}_part", [1, 3, w], BF16) for n, (_, w, _) in rows.items()}
        rest = {n: sb(f"w_{n}_rest", [1, 2, w], FP32) for n, (_, w, _) in rows.items()}
        w_in, centred, split, rows_out = sem("w_in"), sem("w_centred"), sem("w_split"), sem("w_rows_out")
        zeroed, made = sem("w_zeroed"), sem("w_made")
        loads = [
            (k.w1a_x[:], k.W1a[0:C, :]), (k.w1a_e[:], k.W1a[C:2 * C, :]),
            (k.w1b_c[:], k.W1b.rearrange("(h p) n -> p h n", p=P)),
            (k.w2a_x[:], k.W2a[0:C, :]), (k.w2a_g[:], k.W2a[C:2 * C, :]),
            (k.w2b_c[:], k.W2b.rearrange("(h p) n -> p h n", p=P)),
            (k.gn1a[:, 0, :], k.g1a_w.rearrange("(h p) -> p h", p=P)), (k.gn1a[:, 1, :], k.g1a_b.rearrange("(h p) -> p h", p=P)),
            (k.gn2a[:, 0, :], k.g2a_w.rearrange("(h p) -> p h", p=P)), (k.gn2a[:, 1, :], k.g2a_b.rearrange("(h p) -> p h", p=P)),
            (k.b1a_all[:], k.b1a.partition_broadcast(P)), (k.bias0_all[:], k.bias0.partition_broadcast(P)),
        ] + [(d[:, j, :], s.partition_broadcast(P)) for d, s in ((k.g1b_w_all, k.g1b_w), (k.g1b_b_all, k.g1b_b)) for j in range(QT)] \
          + [(row[n][:], rows[n][0].unsqueeze(0)) for n in rows]
        block = ctx.enter_context(nc.Block())

        @block.sync
        def _(sp):
            with nc.allow_non_contiguous_dma("per-channel columns of the norms, once"):
                for to, source in loads:
                    sp.dma_start(to, source).then_inc(w_in, 16)
            sp.wait_ge(split, 5 * len(rows))
            for n, to in (("b1b", k.b1b_row), ("b2a", k.b2a_row), ("b2b", k.b2b_row)):
                for i in range(3):
                    sp.dma_start(to[i:i + 1, :], part[n][0:1, i, :]).then_inc(rows_out, 16)
            sp.wait_ge(rows_out, 16 * 3 * len(rows))

        @block.gpsimd
        def _(pool):
            identity(nc, pool, k.eye[:], zeroed, made)
            nc.gpsimd.memset(k.ones3[:], 1.0).then_inc(made, 1)
            nc.gpsimd.memset(k.eps[:], EPS).then_inc(made, 1)

        @block.vector
        def _(dve):
            dve.wait_ge(w_in, 16 * len(loads))
            at = 0
            both = [(k.w1a_x[:], P), (k.w1a_e[:], P), (k.w1b_c[:, 0, :], P), (k.w1b_c[:, 1, :], P), (k.w2a_x[:], P),
                    (k.w2a_g[:], P), (k.b1a_all[:], P)] + [(row[n][:], 1) for n in rows if rows[n][2]]
            for w, parts in both:
                v = w.rearrange("p (g k) -> p g k", g=G)
                m = mean[0:parts, :]
                nc.vector.tensor_reduce(m, v, AX.X, ALU.add).then_inc(centred, 1)
                dve.wait_ge(centred, at + 1)
                nc.vector.tensor_scalar(m, m, 1.0 / v.shape[2], None, ALU.mult).then_inc(centred, 1)
                dve.wait_ge(centred, at + 2)
                nc.vector.tensor_tensor(v, v, spread(m, parts, v.shape[2]), ALU.subtract).then_inc(centred, 1)
                dve.wait_ge(centred, at + 3)
                at += 3
            at = 0
            for n in rows:
                a, b, r, p3 = row[n][:], None, rest[n], part[n]
                nc.vector.tensor_copy(p3[:, 0, :], a).then_inc(split, 1)
                dve.wait_ge(split, at + 1)
                nc.vector.tensor_tensor(r[:, 0, :], a, p3[:, 0, :], ALU.subtract).then_inc(split, 1)
                dve.wait_ge(split, at + 2)
                nc.vector.tensor_copy(p3[:, 1, :], r[:, 0, :]).then_inc(split, 1)
                dve.wait_ge(split, at + 3)
                nc.vector.tensor_tensor(r[:, 1, :], r[:, 0, :], p3[:, 1, :], ALU.subtract).then_inc(split, 1)
                dve.wait_ge(split, at + 4)
                nc.vector.tensor_copy(p3[:, 2, :], r[:, 1, :]).then_inc(split, 1)
                at += 5


def compare_keys(nc, keys_row, key_f, q, eq, s):
    for j in range(QT):
        last = nc.vector.tensor_scalar(eq[:, j, :], keys_row[:, j * P:(j + 1) * P], key_f[:, bass.ds(q * QT + j, 1)],
                                       None, ALU.is_equal)
    last.then_inc(s, 1)


def first_of_key(nc, dve, q, lower, eq, before, key_f, key_trash, dup, mixed, idx, s_before, s_dup, s_mixed, s_idx):
    nc.vector.tensor_tensor(before, eq, lower.unsqueeze(1).broadcast_to((P, QT, P)), ALU.mult).then_inc(s_before, 1)
    dve.wait_ge(s_before, q + 1)
    nc.vector.tensor_reduce(dup, before, AX.X, ALU.max).then_inc(s_dup, 1)
    dve.wait_ge(s_dup, q + 1)
    nc.vector.tensor_tensor(mixed, dup, key_trash[:, bass.ds(q * QT, QT)], ALU.mult).then_inc(s_mixed, 1)
    dve.wait_ge(s_mixed, q + 1)
    nc.vector.tensor_tensor(idx, mixed, key_f[:, bass.ds(q * QT, QT)], ALU.add).then_inc(s_idx, 1)


def phase_edges0(nc, k):
    GATHER, KEYS, MERGE, SCATTER = 0, 2, 2, 3
    LAG = 4
    with ExitStack() as ctx:
        sb = lambda n, s, d: ctx.enter_context(nc.sbuf_tensor(n, s, d))
        sem = lambda n: ctx.enter_context(nc.semaphore(n))
        y_idx = sb("e0_y_idx", [P, RING, QT], I32)
        vals = sb("e0_vals", [P, RING, QT, C], FP32)
        keys = sb("e0_keys", [P, RING, QE], I32)
        eq = sb("e0_eq", [P, RING, QT, P], FP32)
        before = sb("e0_before", [P, QT, P], FP32)
        dup = sb("e0_dup", [P, QT], FP32)
        mixed = sb("e0_mixed", [P, QT], FP32)
        idx = sb("e0_idx", [P, RING, QT], I32)
        merged = sb("e0_merged", [P, RING, QT, C], FP32)
        ps = ctx.enter_context(nc.psum_tensor("e0_ps", [P, RING, QT, C], FP32))
        y_ready, eq_ready, before_ready, dup_ready, mixed_ready, idx_ready, sum_ready, out_ready = (
            sem(f"e0_{n}") for n in ("y_idx_ready", "eq_ready", "before", "dup", "mixed", "idx_ready", "sum_ready", "out_ready"))
        gathered = [sem(f"e0_gathered{i}") for i in range(RING)]
        keys_in = [sem(f"e0_keys_in{i}") for i in range(RING)]
        added = [sem(f"e0_added{i}") for i in range(KC)]
        issued = sem("e0_issued")
        block = ctx.enter_context(nc.Block())

        @block.sync
        def _(sp):
            for slot, at in pipeline(sp, Q, 0):
                q = at(0)
                if had(q, RING):
                    sp.wait_ge(eq_ready, q - 1)
                sp.dma_start(keys[:, slot, :], k.src_row[bass.ds(q * QE, QE)].partition_broadcast(P)).then_inc(keys_in[slot], 16)

        @block.gpsimd
        def _(pool):
            for slot, at in pipeline(pool, Q, LAG):
                if (q := at(GATHER)) is not None:
                    pool.wait_ge(y_ready, q + 1)
                    if had(q, RING):
                        pool.wait_ge(sum_ready, q - 1)
                    pool.sem_inc(issued, 1)
                    for j in range(QT):
                        nc.gpsimd.indirect_dma_start(vals[:, slot, j, :], None, k.y.rearrange("n (r c) -> (n r) c", r=R),
                                                     bass.IndirectOffsetOnAxis(ap=y_idx[:, slot, j:j + 1], axis=0)).then_inc(gathered[slot], 16)
                if (q := at(SCATTER)) is not None:
                    s = (slot + SCATTER) % RING
                    pool.wait_ge(out_ready, q + 1)
                    pool.wait_ge(idx_ready, q + 1)
                    if had(q, 1):
                        for j in range(QT):
                            pool.wait_ge(added[j], q * 16)
                    pool.sem_inc(issued, 1)
                    for j in range(QT):
                        nc.gpsimd.indirect_dma_start(k.sums0[j], bass.IndirectOffsetOnAxis(ap=idx[:, s, j:j + 1], axis=0),
                                                     merged[:, s, j, :], None, compute_op=ALU.add).then_inc(added[j], 16)
            for j in range(QT):
                pool.wait_ge(added[j], 16 * Q)

        @block.vector
        def _(dve):
            for slot, at in pipeline(dve, Q, LAG):
                if (q := at(GATHER)) is not None:
                    if had(q, RING):
                        dve.wait_ge(gathered[slot], uses(q - RING, slot, 16 * QT))
                    nc.vector.scalar_tensor_tensor(out=y_idx[:, slot, :], in0=k.dst_f[:, bass.ds(q * QT, QT)], scalar=float(R),
                                                   in1=k.type_i[:, bass.ds(q * QT, QT)], op0=ALU.mult, op1=ALU.add).then_inc(y_ready, 1)
                if (q := at(KEYS)) is not None:
                    s = (slot + KEYS) % RING
                    dve.wait_ge(keys_in[s], uses(q, s, 16))
                    if had(q, RING):
                        dve.wait_ge(sum_ready, q - 1)
                        for j in range(QT):
                            dve.wait_ge(added[j], q * 16 - 16)
                    compare_keys(nc, keys[:, s, :], k.src_f, q, eq[:, s], eq_ready)
                    dve.wait_ge(eq_ready, q + 1)
                    first_of_key(nc, dve, q, k.lower[:], eq[:, s], before[:], k.src_f, k.src_trash, dup[:], mixed[:],
                                 idx[:, s, :], before_ready, dup_ready, mixed_ready, idx_ready)

        @block.tensor
        def _(pe):
            for slot, at in pipeline(pe, Q, 0):
                q = at(0)
                pe.wait_ge(gathered[slot], uses(q, slot, 16 * QT))
                pe.wait_ge(eq_ready, q + 1)
                if had(q, RING):
                    pe.wait_ge(out_ready, q - 1)
                for j in range(QT):
                    last = nc.tensor.matmul(ps[:, slot, j, :], eq[:, slot, j, :], vals[:, slot, j, :], start=True, stop=True)
                last.then_inc(sum_ready, 1)

        @block.scalar
        def _(act):
            for slot, at in pipeline(act, Q, 0):
                q = at(0)
                act.wait_ge(sum_ready, q + 1)
                if had(q, RING):
                    for j in range(QT):
                        act.wait_ge(added[j], q * 16 - 16)
                nc.scalar.copy(merged[:, slot].rearrange("p j c -> p (j c)"), ps[:, slot].rearrange("p j c -> p (j c)")).then_inc(out_ready, 1)


def node_rows(table, b):
    return table[bass.ds(b * BN, BN), :].rearrange("(p j) c -> p j c", j=NB)


class Chain:

    def __init__(self, eng, s, steps, b):
        self.eng, self.s, self.n = eng, s, b * steps

    def then(self, instruction):
        instruction.then_inc(self.s, 1)
        self.n = self.n + 1
        self.eng.wait_ge(self.s, self.n)


def phase_nodes1(nc, k):
    with ExitStack() as ctx:
        sb = lambda n, s, d: ctx.enter_context(nc.sbuf_tensor(n, s, d))
        sem = lambda n: ctx.enter_context(nc.semaphore(n))
        x = sb("n1_x", [P, RING, NB, C], FP32)
        sums = sb("n1_sums", [P, RING, KC, NB, C], FP32)
        h = sb("n1_h", [P, NB, C], FP32)
        sq = sb("n1_sq", [P, NB, C], FP32)
        x1 = sb("n1_x1", [P, RING, NB, C], FP32)
        xT = sb("n1_xT", [P, RING, NB, P], FP32)
        xa = sb("n1_xa", [P, RING, NB, H], FP32)
        mean, ss, sd, rs = (sb(f"n1_{n}", [P, NB], FP32) for n in ("mean", "ss", "sd", "rs"))
        psT = ctx.enter_context(nc.psum_tensor("n1_psT", [P, 2, 4, P], FP32))
        psA = ctx.enter_context(nc.psum_tensor("n1_psA", [P, 4, 2, H], FP32))
        step, centred, squared, var_ready, sd_ready, x1_ready, t_ready, xT_ready, xa_ready, xa_out = (
            sem(f"n1_{n}") for n in ("step", "centred", "squared", "var", "sd", "x1", "t", "xT", "xa", "xa_out"))
        x_in = [sem(f"n1_x_in{i}") for i in range(RING)]
        stored = [sem(f"n1_stored{i}") for i in range(RING)]
        STEPS = KC + 1 + 2 + 1
        block = ctx.enter_context(nc.Block())

        @block.sync
        def _(sp):
            for slot, at in pipeline(sp, BLOCKS, 2):
                if (b := at(0)) is not None:
                    if had(b, RING):
                        sp.wait_ge(centred, b - 1)
                    sp.dma_start(x[:, slot], node_rows(k.x, b)).then_inc(x_in[slot], 16)
                    for c in range(KC):
                        sp.dma_start(sums[:, slot, c], node_rows(k.sums0[c], b)).then_inc(x_in[slot], 16)
                if (b := at(2)) is not None:
                    sp.wait_ge(x1_ready, b + 1)
                    sp.dma_start(node_rows(k.x1, b), x1[:, slot]).then_inc(stored[slot], 16)
                    sp.wait_ge(xT_ready, b + 1)
                    sp.dma_start(k.x1T[bass.ds(b, 1)].rearrange("a p m -> (a p) m"), xT[:, slot].rearrange("p j n -> p (j n)")).then_inc(stored[slot], 16)
                    sp.wait_ge(xa_out, b + 1)
                    sp.dma_start(node_rows(k.xa, b), xa[:, slot]).then_inc(stored[slot], 16)
            for slot in range(RING):
                sp.wait_ge(stored[slot], 48 * (BLOCKS // RING))

        @block.vector
        def _(dve):
            for slot, at in pipeline(dve, BLOCKS, 0):
                b = at(0)
                dve.wait_ge(x_in[slot], uses(b, slot, 16 * (KC + 1)))
                if had(b, RING):
                    dve.wait_ge(stored[slot], uses(b - RING, slot, 48))
                chain = Chain(dve, step, STEPS, b)
                chain.then(nc.vector.tensor_tensor(h[:], x[:, slot], k.bias0_all[:].unsqueeze(1).broadcast_to((P, NB, C)), ALU.add))
                for c in range(KC):
                    chain.then(nc.vector.tensor_tensor(h[:], h[:], sums[:, slot, c], ALU.add))
                chain.then(nc.vector.tensor_reduce(mean[:], h[:], AX.X, ALU.add))
                chain.then(nc.vector.tensor_scalar(mean[:], mean[:], 1.0 / C, None, ALU.mult))
                nc.vector.tensor_tensor(h[:], h[:], spread(mean[:], P, C), ALU.subtract).then_inc(centred, 1)
                dve.wait_ge(squared, b + 1)
                nc.vector.tensor_reduce(ss[:], sq[:], AX.X, ALU.add).then_inc(var_ready, 1)
                dve.wait_ge(sd_ready, b + 1)
                chain.then(nc.vector.reciprocal(rs[:], sd[:]))
                if had(b, RING):
                    dve.wait_ge(t_ready, b - 1)
                nc.vector.tensor_tensor(x1[:, slot], h[:], spread(rs[:], P, C), ALU.mult).then_inc(x1_ready, 1)
                dve.wait_ge(xa_ready, b + 1)
                for i, n in ((0, 4), (1, NB - 4)):
                    out = nc.vector.tensor_tensor(xa[:, slot, 4 * i:4 * i + n], psA[:].rearrange("p a b h -> p (a b) h")[:, 4 * i:4 * i + n],
                                                  k.b1a_all[:].unsqueeze(1).broadcast_to((P, n, H)), ALU.add)
                out.then_inc(xa_out, 1)

        @block.scalar
        def _(act):
            for slot, at in pipeline(act, BLOCKS, 0):
                b = at(0)
                act.wait_ge(centred, b + 1)
                nc.scalar.activation(sq[:], h[:], ACT.Square).then_inc(squared, 1)
                act.wait_ge(var_ready, b + 1)
                nc.scalar.activation(sd[:], ss[:], ACT.Sqrt, bias=k.eps[:], scale=1.0 / C).then_inc(sd_ready, 1)
                act.wait_ge(t_ready, b + 1)
                if had(b, RING):
                    act.wait_ge(stored[slot], uses(b - RING, slot, 48))
                flat = psT[:].rearrange("p a b n -> p (a b) n")
                nc.scalar.copy(xT[:, slot], flat[:, 0:NB]).then_inc(xT_ready, 1)

        @block.tensor
        def _(pe):
            for slot, at in pipeline(pe, BLOCKS, 0):
                b = at(0)
                pe.wait_ge(x1_ready, b + 1)
                if had(b, 1):
                    pe.wait_ge(xT_ready, b)
                for j in range(NB):
                    last = nc.tensor.transpose(psT[:, j // 4, j % 4, :], x1[:, slot, j, :], k.eye[:])
                last.then_inc(t_ready, 1)
                pe.wait_ge(xT_ready, b + 1)
                if had(b, 1):
                    pe.wait_ge(xa_out, b)
                for j in range(NB):
                    last = nc.tensor.matmul(psA[:, j // 2, j % 2, :], xT[:, slot, j, :], k.w1a_x[:], start=True, stop=True)
                last.then_inc(xa_ready, 1)


def phase_edges1(nc, k):
    LOAD, A, GN_A, T_B, GN_B, RELU_B, MERGE, SCATTER = 0, 2, 3, 4, 5, 5, 6, 7
    LAG = 8
    with ExitStack() as ctx:
        sb = lambda n, s, d: ctx.enter_context(nc.sbuf_tensor(n, s, d))
        sem = lambda n: ctx.enter_context(nc.semaphore(n))
        pb = lambda n, s: ctx.enter_context(nc.psum_tensor(n, s, FP32))
        ea = sb("e1_ea", [P, RING, QT, P], FP32)
        xa_idx = sb("e1_xa_idx", [P, RING, QT], I32)
        xa = sb("e1_xa", [P, RING, QT, H], FP32)
        sq_a = sb("e1_sq_a", [P, RING, QT * H], FP32)
        norm_a = sb("e1_norm_a", [P, RING, QT, H], FP32)
        hT = sb("e1_hT", [P, RING, 2, QT, P], FP32)
        sq_b = sb("e1_sq_b", [P, RING, QE], FP32)
        norm_b = sb("e1_norm_b", [P, RING, QE], FP32)
        h = sb("e1_h", [P, RING, QT, C], FP32)
        ss_a, sd_a, rs_a, ss_b, sd_b, rs_b = (sb(f"e1_{n}", [P, RING, QT * G], FP32) for n in ("ss_a", "sd_a", "rs_a", "ss_b", "sd_b", "rs_b"))
        keys = sb("e1_keys", [P, RING, QE], I32)
        eq = sb("e1_eq", [P, RING, QT, P], FP32)
        before = sb("e1_before", [P, QT, P], FP32)
        dup = sb("e1_dup", [P, QT], FP32)
        mixed = sb("e1_mixed", [P, QT], FP32)
        idx = sb("e1_idx", [P, RING, QT], I32)
        merged = sb("e1_merged", [P, RING, QT, SW], FP32)
        psA, psT, psB, psM = pb("e1_psA", [P, RING, QT, H]), pb("e1_psT", [P, 2, QT, P]), pb("e1_psB", [P, QT, C]), pb("e1_psM", [P, QT, C])
        S = {n: sem(f"e1_{n}_ready") for n in ("xa_idx", "a", "sq_a", "ss_a", "sd_a", "rs_a", "norm_a", "t", "hT", "b", "sq_b", "ss_b", "sd_b", "rs_b", "norm_b",
                  "scaled", "shifted", "h", "eq", "before", "dup", "mixed", "idx", "counted", "sum", "out")}
        ea_in = [sem(f"e1_ea_in{i}") for i in range(RING)]
        keys_in = [sem(f"e1_keys_in{i}") for i in range(RING)]
        gathered = [sem(f"e1_gathered{i}") for i in range(RING)]
        added = [sem(f"e1_added{i}") for i in range(KC)]
        issued = sem("e1_issued")
        block = ctx.enter_context(nc.Block())
        at_slot = lambda slot, lag: (slot + lag) % RING

        @block.sync
        def _(sp):
            for slot, at in pipeline(sp, Q, 4):
                if (q := at(LOAD)) is not None:
                    if had(q, RING):
                        sp.wait_ge(S["a"], q - 1)
                    sp.dma_start(ea[:, slot].rearrange("p j e -> p (j e)"), k.ea_T[:, bass.ds(q * QE, QE)]).then_inc(ea_in[slot], 16)
                if (q := at(4)) is not None:
                    if had(q, RING):
                        sp.wait_ge(S["eq"], q - 1)
                    sp.dma_start(keys[:, slot, :], k.dst_row[bass.ds(q * QE, QE)].partition_broadcast(P)).then_inc(keys_in[slot], 16)

        @block.gpsimd
        def _(pool):
            for slot, at in pipeline(pool, Q, LAG):
                if (q := at(LOAD)) is not None:
                    pool.wait_ge(S["xa_idx"], q + 1)
                    if had(q, RING):
                        pool.wait_ge(S["a"], q - 1)
                    pool.sem_inc(issued, 1)
                    for j in range(QT):
                        nc.gpsimd.indirect_dma_start(xa[:, slot, j, :], None, k.xa,
                                                     bass.IndirectOffsetOnAxis(ap=xa_idx[:, slot, j:j + 1], axis=0)).then_inc(gathered[slot], 16)
                if (q := at(SCATTER)) is not None:
                    s = at_slot(slot, SCATTER)
                    pool.wait_ge(S["out"], q + 1)
                    pool.wait_ge(S["counted"], q + 1)
                    pool.wait_ge(S["idx"], q + 1)
                    if had(q, 1):
                        for j in range(QT):
                            pool.wait_ge(added[j], q * 16)
                    pool.sem_inc(issued, 1)
                    for j in range(QT):
                        nc.gpsimd.indirect_dma_start(k.sums1[j], bass.IndirectOffsetOnAxis(ap=idx[:, s, j:j + 1], axis=0),
                                                     merged[:, s, j, :], None, compute_op=ALU.add).then_inc(added[j], 16)
            for j in range(QT):
                pool.wait_ge(added[j], 16 * Q)

        @block.tensor
        def _(pe):
            for slot, at in pipeline(pe, Q, 6):
                if (q := at(T_B)) is not None:
                    s = at_slot(slot, T_B)
                    pe.wait_ge(S["norm_a"], q + 1)
                    if had(q, 1):
                        pe.wait_ge(S["hT"], q)
                    for half in range(2):
                        for j in range(QT):
                            last = nc.tensor.transpose(psT[:, half, j, :], norm_a[:, s, j, half * P:(half + 1) * P], k.eye[:])
                    last.then_inc(S["t"], 1)
                if (q := at(MERGE)) is not None:
                    s = at_slot(slot, MERGE)
                    pe.wait_ge(S["h"], q + 1)
                    pe.wait_ge(S["eq"], q + 1)
                    if had(q, 1):
                        pe.wait_ge(S["out"], q)
                    for j in range(QT):
                        last = nc.tensor.matmul(psM[:, j, :], eq[:, s, j, :], h[:, s, j, :], start=True, stop=True)
                    last.then_inc(S["sum"], 1)
                if (q := at(A)) is not None:
                    s = at_slot(slot, A)
                    pe.wait_ge(ea_in[s], uses(q, s, 16))
                    pe.wait_ge(gathered[s], uses(q, s, 16 * QT))
                    if had(q, RING):
                        pe.wait_ge(S["norm_a"], q - 1)
                    for j in range(QT):
                        nc.tensor.matmul(psA[:, s, j, :], ea[:, s, j, :], k.w1a_e[:], start=True, stop=False)
                        last = nc.tensor.matmul(psA[:, s, j, :], k.eye[:], xa[:, s, j, :], start=False, stop=True)
                    last.then_inc(S["a"], 1)
                if (q := at(T_B)) is not None:
                    s = at_slot(slot, T_B)
                    pe.wait_ge(S["hT"], q + 1)
                    if had(q, 1):
                        pe.wait_ge(S["norm_b"], q)
                    for j in range(QT):
                        nc.tensor.matmul(psB[:, j, :], k.ones3[:], k.b1b_row[:], start=True, stop=False)
                        nc.tensor.matmul(psB[:, j, :], hT[:, s, 0, j, :], k.w1b_c[:, 0, :], start=False, stop=False)
                        last = nc.tensor.matmul(psB[:, j, :], hT[:, s, 1, j, :], k.w1b_c[:, 1, :], start=False, stop=True)
                    last.then_inc(S["b"], 1)

        @block.scalar
        def _(act):
            flat = lambda x: x.rearrange("p j c -> p (j c)")
            for slot, at in pipeline(act, Q, 6):
                if (q := at(GN_B)) is not None:
                    s = at_slot(slot, GN_B)
                    act.wait_ge(S["b"], q + 1)
                    if had(q, RING):
                        act.wait_ge(S["ss_b"], q - 1)
                    nc.scalar.activation(sq_b[:, s, :], flat(psB[:]), ACT.Square).then_inc(S["sq_b"], 1)
                if (q := at(T_B)) is not None:
                    s = at_slot(slot, T_B)
                    act.wait_ge(S["t"], q + 1)
                    if had(q, RING):
                        act.wait_ge(S["b"], q - 1)
                    for half in range(2):
                        last = nc.scalar.activation(flat(hT[:, s, half]), flat(psT[:, half]), ACT.Relu,
                                                    bias=k.gn1a[:, 1, half:half + 1], scale=k.gn1a[:, 0, half:half + 1])
                    last.then_inc(S["hT"], 1)
                if (q := at(GN_A)) is not None:
                    s = at_slot(slot, GN_A)
                    act.wait_ge(S["ss_a"], q + 1)
                    if had(q, RING):
                        act.wait_ge(S["rs_a"], q - 1)
                    nc.scalar.activation(sd_a[:, s, :], ss_a[:, s, :], ACT.Sqrt, bias=k.eps[:], scale=float(G) / H).then_inc(S["sd_a"], 1)
                if (q := at(GN_B)) is not None:
                    s = at_slot(slot, GN_B)
                    act.wait_ge(S["ss_b"], q + 1)
                    if had(q, RING):
                        act.wait_ge(S["rs_b"], q - 1)
                    nc.scalar.activation(sd_b[:, s, :], ss_b[:, s, :], ACT.Sqrt, bias=k.eps[:], scale=float(G) / C).then_inc(S["sd_b"], 1)
                if (q := at(A)) is not None:
                    s = at_slot(slot, A)
                    act.wait_ge(S["a"], q + 1)
                    if had(q, RING):
                        act.wait_ge(S["ss_a"], q - 1)
                    nc.scalar.activation(sq_a[:, s, :], flat(psA[:, s]), ACT.Square).then_inc(S["sq_a"], 1)
                if (q := at(RELU_B)) is not None:
                    s = at_slot(slot, RELU_B)
                    act.wait_ge(S["shifted"], q + 1)
                    if had(q, RING):
                        act.wait_ge(S["sum"], q - 1)
                    nc.scalar.activation(flat(h[:, s]), norm_b[:, s, :], ACT.Relu).then_inc(S["h"], 1)
                if (q := at(MERGE)) is not None:
                    s = at_slot(slot, MERGE)
                    act.wait_ge(S["sum"], q + 1)
                    if had(q, RING):
                        for j in range(QT):
                            act.wait_ge(added[j], q * 16 - 16)
                    nc.scalar.copy(merged[:, s, :, 0:C], psM[:]).then_inc(S["out"], 1)

        @block.vector
        def _(dve):
            groups = lambda x, n: x.rearrange("p (g k) -> p g k", g=n)
            for slot, at in pipeline(dve, Q, 6):
                if (q := at(LOAD)) is not None:
                    if had(q, RING):
                        dve.wait_ge(gathered[slot], uses(q - RING, slot, 16 * QT))
                    nc.vector.tensor_copy(xa_idx[:, slot, :], k.src_idx[:, bass.ds(q * QT, QT)]).then_inc(S["xa_idx"], 1)
                if (q := at(GN_B)) is not None:
                    s = at_slot(slot, GN_B)
                    dve.wait_ge(S["sq_b"], q + 1)
                    if had(q, RING):
                        dve.wait_ge(S["sd_b"], q - 1)
                    nc.vector.tensor_reduce(ss_b[:, s, :], groups(sq_b[:, s, :], QT * G), AX.X, ALU.add).then_inc(S["ss_b"], 1)
                if (q := at(GN_A)) is not None:
                    s = at_slot(slot, GN_A)
                    dve.wait_ge(S["sq_a"], q + 1)
                    if had(q, RING):
                        dve.wait_ge(S["sd_a"], q - 1)
                    nc.vector.tensor_reduce(ss_a[:, s, :], groups(sq_a[:, s, :], QT * G), AX.X, ALU.add).then_inc(S["ss_a"], 1)
                if (q := at(GN_B)) is not None:
                    s = at_slot(slot, GN_B)
                    dve.wait_ge(S["sd_b"], q + 1)
                    nc.vector.reciprocal(rs_b[:, s, :], sd_b[:, s, :]).then_inc(S["rs_b"], 1)
                    dve.wait_ge(S["rs_b"], q + 1)
                    if had(q, RING):
                        dve.wait_ge(S["h"], q - 1)
                    nc.vector.tensor_tensor(groups(norm_b[:, s, :], QT * G), psB[:].rearrange("p j (g k) -> p (j g) k", g=G),
                                            spread(rs_b[:, s, :], P, C // G), ALU.mult).then_inc(S["norm_b"], 1)
                    dve.wait_ge(S["norm_b"], q + 1)
                    nc.vector.tensor_tensor(norm_b[:, s, :], norm_b[:, s, :], k.g1b_w_all[:].rearrange("p j c -> p (j c)"),
                                            ALU.mult).then_inc(S["scaled"], 1)
                    dve.wait_ge(S["scaled"], q + 1)
                    nc.vector.tensor_tensor(norm_b[:, s, :], norm_b[:, s, :], k.g1b_b_all[:].rearrange("p j c -> p (j c)"),
                                            ALU.add).then_inc(S["shifted"], 1)
                if (q := at(GN_A)) is not None:
                    s = at_slot(slot, GN_A)
                    dve.wait_ge(S["sd_a"], q + 1)
                    nc.vector.reciprocal(rs_a[:, s, :], sd_a[:, s, :]).then_inc(S["rs_a"], 1)
                    dve.wait_ge(S["rs_a"], q + 1)
                    if had(q, RING):
                        dve.wait_ge(S["t"], q - 1)
                    nc.vector.tensor_tensor(norm_a[:, s].rearrange("p j (g k) -> p (j g) k", g=G), psA[:, s].rearrange("p j (g k) -> p (j g) k", g=G),
                                            spread(rs_a[:, s, :], P, H // G), ALU.mult).then_inc(S["norm_a"], 1)
                if (q := at(GN_B)) is not None:
                    s = at_slot(slot, GN_B)
                    dve.wait_ge(keys_in[s], uses(q, s, 16))
                    if had(q, RING):
                        dve.wait_ge(S["sum"], q - 1)
                        for j in range(QT):
                            dve.wait_ge(added[j], q * 16 - 16)
                    compare_keys(nc, keys[:, s, :], k.dst_f, q, eq[:, s], S["eq"])
                    dve.wait_ge(S["eq"], q + 1)
                    nc.vector.tensor_reduce(merged[:, s, :, C:SW], eq[:, s], AX.X, ALU.add).then_inc(S["counted"], 1)
                    first_of_key(nc, dve, q, k.lower[:], eq[:, s], before[:], k.dst_f, k.dst_trash, dup[:], mixed[:],
                                 idx[:, s, :], S["before"], S["dup"], S["mixed"], S["idx"])


def phase_nodes2(nc, k):
    with ExitStack() as ctx:
        sb = lambda n, s, d: ctx.enter_context(nc.sbuf_tensor(n, s, d))
        sem = lambda n: ctx.enter_context(nc.semaphore(n))
        sums = sb("n2_sums", [P, RING, KC, NB, SW], FP32)
        x1 = sb("n2_x1", [P, RING, NB, C], FP32)
        xT = sb("n2_xT", [P, RING, NB, P], FP32)
        total = sb("n2_total", [P, NB, SW], FP32)
        agg = sb("n2_agg", [P, NB, C], FP32)
        aggT = sb("n2_aggT", [P, NB, P], FP32)
        sq = sb("n2_sq", [P, NB, H], FP32)
        norm = sb("n2_norm", [P, NB, H], FP32)
        hT = sb("n2_hT", [P, 2, NB, P], FP32)
        z = sb("n2_z", [P, NB, C], FP32)
        out = sb("n2_out", [P, RING, NB, C], FP32)
        cnt, mean, ss2, sd2, rs2 = (sb(f"n2_{n}", [P, NB], FP32) for n in ("cnt", "mean", "ss2", "sd2", "rs2"))
        ss, sd, rs = (sb(f"n2_{n}", [P, NB * G], FP32) for n in ("ss", "sd", "rs"))
        psT = ctx.enter_context(nc.psum_tensor("n2_psT", [P, 8, P], FP32))
        psU = ctx.enter_context(nc.psum_tensor("n2_psU", [P, 8, H], FP32))
        psH = psU[:].rearrange("p a (b n) -> p (a b) n", b=2)
        S = {n: sem(f"n2_{n}_ready") for n in ("step", "agg", "t", "aggT", "u", "sq", "ss", "sd", "norm", "th", "hT", "z", "centred", "sq2", "ss2", "sd2", "out")}
        loaded = [sem(f"n2_loaded{i}") for i in range(RING)]
        stored = [sem(f"n2_stored{i}") for i in range(RING)]
        STEPS = KC - 1 + 2 + 1 + 1 + 2 + 1
        block = ctx.enter_context(nc.Block())

        @block.sync
        def _(sp):
            for slot, at in pipeline(sp, BLOCKS, 2):
                if (b := at(0)) is not None:
                    if had(b, RING):
                        sp.wait_ge(S["out"], b - 1)
                    for c in range(KC):
                        sp.dma_start(sums[:, slot, c], node_rows(k.sums1[c], b)).then_inc(loaded[slot], 16)
                    sp.dma_start(x1[:, slot], node_rows(k.x1, b)).then_inc(loaded[slot], 16)
                    sp.dma_start(xT[:, slot].rearrange("p j n -> p (j n)"), k.x1T[bass.ds(b, 1)].rearrange("a p m -> (a p) m")).then_inc(loaded[slot], 16)
                if (b := at(2)) is not None:
                    sp.wait_ge(S["out"], b + 1)
                    sp.dma_start(node_rows(k.out, b), out[:, slot]).then_inc(stored[slot], 16)
            for slot in range(RING):
                sp.wait_ge(stored[slot], 16 * (BLOCKS // RING))

        @block.vector
        def _(dve):
            for slot, at in pipeline(dve, BLOCKS, 0):
                b = at(0)
                dve.wait_ge(loaded[slot], uses(b, slot, 16 * (KC + 2)))
                chain = Chain(dve, S["step"], STEPS, b)
                chain.then(nc.vector.tensor_tensor(total[:], sums[:, slot, 0], sums[:, slot, 1], ALU.add))
                for c in range(2, KC):
                    chain.then(nc.vector.tensor_tensor(total[:], total[:], sums[:, slot, c], ALU.add))
                chain.then(nc.vector.tensor_scalar(cnt[:], total[:, :, C], 1.0, None, ALU.max))
                chain.then(nc.vector.reciprocal(cnt[:], cnt[:]))
                if had(b, 1):
                    dve.wait_ge(S["t"], b)
                nc.vector.tensor_tensor(agg[:], total[:, :, 0:C], spread(cnt[:], P, C), ALU.mult).then_inc(S["agg"], 1)
                dve.wait_ge(S["sq"], b + 1)
                nc.vector.tensor_reduce(ss[:], sq[:].rearrange("p j (g k) -> p (j g) k", g=G), AX.X, ALU.add).then_inc(S["ss"], 1)
                dve.wait_ge(S["sd"], b + 1)
                chain.then(nc.vector.reciprocal(rs[:], sd[:]))
                nc.vector.tensor_tensor(norm[:].rearrange("p j (g k) -> p (j g) k", g=G), psU[:, 0:NB, :].rearrange("p j (g k) -> p (j g) k", g=G),
                                        spread(rs[:], P, H // G), ALU.mult).then_inc(S["norm"], 1)
                dve.wait_ge(S["z"], b + 1)
                chain.then(nc.vector.tensor_tensor(z[:], psT[:, 0:NB, :], x1[:, slot], ALU.add))
                chain.then(nc.vector.tensor_reduce(mean[:], z[:], AX.X, ALU.add))
                chain.then(nc.vector.tensor_scalar(mean[:], mean[:], 1.0 / C, None, ALU.mult))
                nc.vector.tensor_tensor(z[:], z[:], spread(mean[:], P, C), ALU.subtract).then_inc(S["centred"], 1)
                dve.wait_ge(S["sq2"], b + 1)
                nc.vector.tensor_reduce(ss2[:], sq[:, :, 0:C], AX.X, ALU.add).then_inc(S["ss2"], 1)
                dve.wait_ge(S["sd2"], b + 1)
                chain.then(nc.vector.reciprocal(rs2[:], sd2[:]))
                if had(b, RING):
                    dve.wait_ge(stored[slot], uses(b - RING, slot, 16))
                nc.vector.tensor_tensor(out[:, slot], z[:], spread(rs2[:], P, C), ALU.mult).then_inc(S["out"], 1)

        @block.scalar
        def _(act):
            for slot, at in pipeline(act, BLOCKS, 0):
                b = at(0)
                act.wait_ge(S["t"], b + 1)
                nc.scalar.copy(aggT[:], psT[:, 0:NB, :]).then_inc(S["aggT"], 1)
                act.wait_ge(S["u"], b + 1)
                nc.scalar.activation(sq[:], psU[:, 0:NB, :], ACT.Square).then_inc(S["sq"], 1)
                act.wait_ge(S["ss"], b + 1)
                nc.scalar.activation(sd[:], ss[:], ACT.Sqrt, bias=k.eps[:], scale=float(G) / H).then_inc(S["sd"], 1)
                act.wait_ge(S["th"], b + 1)
                for half in range(2):
                    last = nc.scalar.activation(hT[:, half], psH[:, half * 8:half * 8 + NB, :], ACT.Relu,
                                                bias=k.gn2a[:, 1, half:half + 1], scale=k.gn2a[:, 0, half:half + 1])
                last.then_inc(S["hT"], 1)
                act.wait_ge(S["centred"], b + 1)
                nc.scalar.activation(sq[:, :, 0:C], z[:], ACT.Square).then_inc(S["sq2"], 1)
                act.wait_ge(S["ss2"], b + 1)
                nc.scalar.activation(sd2[:], ss2[:], ACT.Sqrt, bias=k.eps[:], scale=1.0 / C).then_inc(S["sd2"], 1)

        @block.tensor
        def _(pe):
            for slot, at in pipeline(pe, BLOCKS, 0):
                b = at(0)
                pe.wait_ge(loaded[slot], uses(b, slot, 16 * (KC + 2)))
                pe.wait_ge(S["agg"], b + 1)
                if had(b, 1):
                    pe.wait_ge(S["centred"], b)
                for j in range(NB):
                    last = nc.tensor.transpose(psT[:, j, :], agg[:, j, :], k.eye[:])
                last.then_inc(S["t"], 1)
                pe.wait_ge(S["aggT"], b + 1)
                for j in range(NB):
                    nc.tensor.matmul(psU[:, j, :], k.ones3[:], k.b2a_row[:], start=True, stop=False)
                    nc.tensor.matmul(psU[:, j, :], xT[:, slot, j, :], k.w2a_x[:], start=False, stop=False)
                    last = nc.tensor.matmul(psU[:, j, :], aggT[:, j, :], k.w2a_g[:], start=False, stop=True)
                last.then_inc(S["u"], 1)
                pe.wait_ge(S["norm"], b + 1)
                for half in range(2):
                    for j in range(NB):
                        last = nc.tensor.transpose(psH[:, half * 8 + j, :], norm[:, j, half * P:(half + 1) * P], k.eye[:])
                last.then_inc(S["th"], 1)
                pe.wait_ge(S["hT"], b + 1)
                for j in range(NB):
                    nc.tensor.matmul(psT[:, j, :], k.ones3[:], k.b2b_row[:], start=True, stop=False)
                    nc.tensor.matmul(psT[:, j, :], hT[:, 0, j, :], k.w2b_c[:, 0, :], start=False, stop=False)
                    last = nc.tensor.matmul(psT[:, j, :], hT[:, 1, j, :], k.w2b_c[:, 1, :], start=False, stop=True)
                last.then_inc(S["z"], 1)


def build(nc, k):
    k.y = nc.dram_tensor("y_table", (N, R * C), FP32, kind="Internal").ap()
    k.sums0 = [nc.dram_tensor(f"sums0_{c}", (ROWS, C), FP32, kind="Internal").ap() for c in range(KC)]
    k.sums1 = [nc.dram_tensor(f"sums1_{c}", (ROWS, SW), FP32, kind="Internal").ap() for c in range(KC)]
    k.xa = nc.dram_tensor("xa_table", (N, H), FP32, kind="Internal").ap()
    k.x1 = nc.dram_tensor("x1_table", (N, C), FP32, kind="Internal").ap()
    k.x1T = nc.dram_tensor("x1T_blocks", (BLOCKS, P, BN), FP32, kind="Internal").ap()
    with ExitStack() as ctx:
        sb = lambda n, s, d: ctx.enter_context(nc.sbuf_tensor(n, s, d))
        k.src_idx = sb("src_idx", [P, T], I32)
        k.type_i = sb("type_i", [P, T], I32)
        k.src_f = sb("src_f", [P, T], FP32)
        k.dst_f = sb("dst_f", [P, T], FP32)
        k.src_trash = sb("src_trash", [P, T], FP32)
        k.dst_trash = sb("dst_trash", [P, T], FP32)
        k.lower = sb("lower", [P, P], FP32)
        k.eye = sb("eye", [P, P], FP32)
        k.eps = sb("eps", [P, 1], FP32)
        k.ones3 = sb("ones3", [3, P], BF16)
        k.w1a_x, k.w1a_e, k.w2a_x, k.w2a_g, k.b1a_all = (sb(n, [P, H], FP32) for n in ("w1a_x", "w1a_e", "w2a_x", "w2a_g", "b1a_all"))
        k.w1b_c, k.w2b_c = sb("w1b_c", [P, 2, C], FP32), sb("w2b_c", [P, 2, C], FP32)
        k.gn1a, k.gn2a = sb("gn1a", [P, 2, 2], FP32), sb("gn2a", [P, 2, 2], FP32)
        k.g1b_w_all, k.g1b_b_all = sb("g1b_w_all", [P, QT, C], FP32), sb("g1b_b_all", [P, QT, C], FP32)
        k.bias0_all = sb("bias0_all", [P, C], FP32)
        k.b1b_row, k.b2a_row, k.b2b_row = sb("b1b_row", [3, C], BF16), sb("b2a_row", [3, H], BF16), sb("b2b_row", [3, C], BF16)
        phase_tables(nc, k)
        phase_weights(nc, k)
        phase_edges0(nc, k)
        phase_nodes1(nc, k)
        phase_edges1(nc, k)
        phase_nodes2(nc, k)


def padded(a, rows, fill):
    return np.concatenate([a, np.full((rows - a.shape[0],) + a.shape[1:], fill, a.dtype)])


def kernel(**inputs):
    import concourse.bacc as bacc
    from concourse.bass_utils import run_bass_kernel_spmd

    a = {n: np.asarray(v) for n, v in inputs.items()}
    src, dst = (padded(a[n].astype(np.int32, copy=False), T * P, NODES) for n in ("src", "dst"))
    types = padded(a["edge_type_8"].astype(np.int32, copy=False), T * P, 0)
    x = padded(a["x"], N, 0)
    columns = lambda v: np.ascontiguousarray(v.reshape(T, P).T)
    arrays = {
        "x": x, "x_T": np.ascontiguousarray(x.T), "src_row": src, "dst_row": dst,
        "src_cols": columns(src), "dst_cols": columns(dst), "type_cols": columns(types),
        "ea_T": np.ascontiguousarray(padded(a["edge_attr_128"], T * P, 0).T),
        "w_rel": np.ascontiguousarray(a["L0_gnn_weight"].transpose(1, 0, 2).reshape(C, R * C)),
        "bias0": a["L0_gnn_bias"], "W1a": a["L1_gnn_W1a"], "b1a": a["L1_gnn_b1a"], "W1b": a["L1_gnn_W1b"], "b1b": a["L1_gnn_b1b"],
        "W2a": a["L1_gnn_W2a"], "b2a": a["L1_gnn_b2a"], "W2b": a["L1_gnn_W2b"], "b2b": a["L1_gnn_b2b"],
        "g1a_w": a["L1_gnn_gn1a_w"], "g1a_b": a["L1_gnn_gn1a_b"], "g1b_w": a["L1_gnn_gn1b_w"], "g1b_b": a["L1_gnn_gn1b_b"],
        "g2a_w": a["L1_gnn_gn2a_w"], "g2a_b": a["L1_gnn_gn2a_b"],
    }
    nc = bacc.Bacc("TRN2", target_bir_lowering=False, num_devices=1)
    aps = {n: nc.dram_tensor(f"in_{n}", v.shape, mybir.dt.from_np(v.dtype), kind="ExternalInput").ap() for n, v in arrays.items()}
    k = Names()
    k.x, k.x_T, k.src_row, k.dst_row = (aps[n] for n in ("x", "x_T", "src_row", "dst_row"))
    k.src_cols, k.dst_cols, k.type_cols, k.ea_T = (aps[n] for n in ("src_cols", "dst_cols", "type_cols", "ea_T"))
    k.w_rel, k.bias0 = aps["w_rel"], aps["bias0"]
    k.W1a, k.b1a, k.W1b, k.b1b = (aps[n] for n in ("W1a", "b1a", "W1b", "b1b"))
    k.W2a, k.b2a, k.W2b, k.b2b = (aps[n] for n in ("W2a", "b2a", "W2b", "b2b"))
    k.g1a_w, k.g1a_b, k.g1b_w, k.g1b_b, k.g2a_w, k.g2a_b = (aps[n] for n in ("g1a_w", "g1a_b", "g1b_w", "g1b_b", "g2a_w", "g2a_b"))
    k.out = nc.dram_tensor("out", (N, C), FP32, kind="ExternalOutput").ap()
    build(nc, k)
    r = run_bass_kernel_spmd(nc, [{f"in_{n}": v for n, v in arrays.items()}], core_ids=[0])
    return r.results[0]["out"][0:NODES]
```

```python
from contextlib import ExitStack

import numpy as np
import concourse.bass as bass
from concourse import mybir

FP32, BF16, I32 = mybir.dt.float32, mybir.dt.bfloat16, mybir.dt.int32
ALU, ACT, AX = mybir.AluOpType, mybir.ActivationFunctionType, mybir.AxisListType

P = 128
C = 128
R = 8
H = 256
G = 8
NODES, EDGES = 12500, 212500
EPS = 1e-5
NB = 7
BLOCKS = 14
BN = NB * P
N = BN * BLOCKS
QT = 4
QE = QT * P
T = 1664
Q = T // QT
TRASH = N
ROWS = N + P
K0, K1 = 4, 2
WINDOW = 2 * QE
W = T * P // WINDOW
SW = C + 1
RING = 2
BANK = 512


class Names:
    pass


def pipeline(eng, count, lag):
    head = lag + RING + (lag % 2)
    for s in range(head):
        yield s % RING, lambda L, by=1: (s - L) // by if 0 <= s - L < count else None
    with eng.Fori(head // RING, count // RING) as turn:
        for u in range(RING):
            yield u, lambda L, by=1: turn * (RING // by) + (u - L) // by
    for s in range(count, count + lag):
        yield s % RING, lambda L, by=1: (s - L) // by if 0 <= s - L < count else None


def had(q, n):
    return q - n >= 0 if isinstance(q, int) else True


def uses(q, slot, each):
    return (q - slot) * (each // RING) + each


def identity(nc, pool, eye, zeroed, made):
    nc.gpsimd.memset(eye, 0.0).then_inc(zeroed, 1)
    pool.wait_ge(zeroed, 1)
    nc.gpsimd.affine_select(out=eye, in_=eye, compare_op=ALU.not_equal, fill=1.0, base=0,
                            pattern=[[-1, P]], channel_multiplier=1).then_inc(made, 1)


def spread(per_group, parts, k):
    return per_group.unsqueeze(2).broadcast_to((parts, per_group.shape[1], k))


def phase_tables(nc, k):
    HALF = R * C // 2
    with ExitStack() as ctx:
        sb = lambda n, s, d: ctx.enter_context(nc.sbuf_tensor(n, s, d))
        sem = lambda n: ctx.enter_context(nc.semaphore(n))
        w = sb("t_w", [P, R * C], FP32)
        xT = sb("t_xT", [P, RING, P], FP32)
        y = sb("t_y", [P, RING, R * C], FP32)
        zeros = sb("t_zeros", [P, 1024], FP32)
        dst_i = sb("t_dst_i", [P, T], I32)
        trash = sb("t_trash", [P, 1], FP32)
        trash_i = sb("t_trash_i", [P, 1], I32)
        base_i = sb("t_base_i", [P, W], I32)
        base_f = sb("t_base_f", [P, W], FP32)
        most, least, fits = sb("t_most", [P, 1], FP32), sb("t_least", [P, 1], FP32), sb("t_fits", [P, 1], FP32)
        ones_col = sb("t_ones_col", [P, 1], FP32)
        iota_i = sb("t_iota_i", [P, P], I32)
        ps_fits = ctx.enter_context(nc.psum_tensor("t_ps_fits", [1, 1], FP32))
        ps = ctx.enter_context(nc.psum_tensor("t_ps", [P, RING, R * C], FP32))
        w_in, keys_in, zeroed, zero_out = sem("t_w_in"), sem("t_keys_in"), sem("t_zeroed"), sem("t_zero_out")
        x_in = [sem(f"t_x_in{i}") for i in range(RING)]
        product, copied_a, copied_v = sem("t_product"), sem("t_copied_act"), sem("t_copied_dve")
        stored = [sem(f"t_stored{i}") for i in range(RING)]
        cast, keyed, ones, made, trash_made = sem("t_cast"), sem("t_keyed"), sem("t_ones"), sem("t_made"), sem("t_trash")
        extremes, fit, counted, flagged = sem("t_extremes"), sem("t_fit"), sem("t_fit_counted"), sem("t_flagged")
        tiles = N // P
        block = ctx.enter_context(nc.Block())

        @block.sync
        def _(sp):
            sp.dma_start(w[:], k.w_rel).then_inc(w_in, 16)
            sp.dma_start(k.src_idx[:], k.src_cols).then_inc(keys_in, 16)
            sp.dma_start(dst_i[:], k.dst_cols).then_inc(keys_in, 16)
            sp.dma_start(k.type_i[:], k.type_cols).then_inc(keys_in, 16)
            sp.dma_start(base_i[:], k.base_row.partition_broadcast(P)).then_inc(keys_in, 16)
            sp.dma_start(k.base_i[:], k.base_row.unsqueeze(0)).then_inc(keys_in, 16)
            for slot, at in pipeline(sp, tiles, 2):
                if (t := at(0)) is not None:
                    if had(t, RING):
                        sp.wait_ge(product, t - 1)
                    sp.dma_start(xT[:, slot, :], k.x_T[:, bass.ds(t * P, P)]).then_inc(x_in[slot], 16)
                if (t := at(2)) is not None:
                    sp.wait_ge(copied_a, t + 1)
                    sp.wait_ge(copied_v, t + 1)
                    sp.dma_start(k.y[bass.ds(t * P, P), :], y[:, slot, :]).then_inc(stored[slot], 16)
            for slot in range(RING):
                sp.wait_ge(stored[slot], 16 * (tiles // RING))

        @block.tensor
        def _(pe):
            pe.wait_ge(w_in, 16)
            for slot, at in pipeline(pe, tiles, 0):
                t = at(0)
                pe.wait_ge(x_in[slot], uses(t, slot, 16))
                if had(t, RING):
                    pe.wait_ge(copied_a, t - 1)
                    pe.wait_ge(copied_v, t - 1)
                nc.tensor.matmul(ps[:, slot, 0:HALF], xT[:, slot, :], w[:, 0:HALF], start=True, stop=True)
                nc.tensor.matmul(ps[:, slot, HALF:2 * HALF], xT[:, slot, :], w[:, HALF:2 * HALF],
                                 start=True, stop=True).then_inc(product, 1)
            pe.wait_ge(fit, 2)
            nc.tensor.matmul(ps_fits[:], fits[:], ones_col[:], start=True, stop=True).then_inc(counted, 1)

        @block.scalar
        def _(act):
            for slot, at in pipeline(act, tiles, 0):
                t = at(0)
                act.wait_ge(product, t + 1)
                if had(t, RING):
                    act.wait_ge(stored[slot], uses(t - RING, slot, 16))
                nc.scalar.copy(y[:, slot, 0:HALF], ps[:, slot, 0:HALF]).then_inc(copied_a, 1)

        @block.vector
        def _(dve):
            nc.vector.memset(zeros[:], 0.0).then_inc(zeroed, 1)
            dve.wait_ge(keys_in, 80)
            dve.wait_ge(trash_made, 2)
            nc.vector.tensor_copy(k.src_f[:], k.src_idx[:]).then_inc(cast, 1)
            nc.vector.tensor_copy(k.dst_f[:], dst_i[:]).then_inc(cast, 1)
            nc.vector.tensor_copy(trash[:], trash_i[:]).then_inc(cast, 1)
            nc.vector.tensor_copy(base_f[:], base_i[:]).then_inc(cast, 1)
            nc.vector.tensor_copy(k.iota[:], iota_i[:]).then_inc(cast, 1)
            nc.vector.memset(ones_col[:], 1.0).then_inc(cast, 1)
            dve.wait_ge(cast, 6)
            nc.vector.tensor_scalar(k.src_trash[:], k.src_f[:], -1.0, trash[:], ALU.mult, ALU.add).then_inc(keyed, 1)
            nc.vector.tensor_scalar(k.dst_trash[:], k.dst_f[:], -1.0, trash[:], ALU.mult, ALU.add).then_inc(keyed, 1)
            nc.vector.tensor_tensor(k.rel[:].rearrange("p (w t) -> p w t", w=W), k.dst_f[:].rearrange("p (w t) -> p w t", w=W),
                                    spread(base_f[:], P, T // W), ALU.subtract).then_inc(keyed, 1)
            dve.wait_ge(keyed, 3)
            nc.vector.tensor_reduce(most[:], k.rel[:], AX.X, ALU.max).then_inc(extremes, 1)
            nc.vector.tensor_reduce(least[:], k.rel[:], AX.X, ALU.min).then_inc(extremes, 1)
            dve.wait_ge(extremes, 2)
            nc.vector.tensor_scalar(most[:], most[:], float(P - 1), None, ALU.is_le).then_inc(fit, 1)
            dve.wait_ge(fit, 1)
            nc.vector.scalar_tensor_tensor(out=fits[:], in0=least[:], scalar=0.0, in1=most[:], op0=ALU.is_ge, op1=ALU.mult).then_inc(fit, 1)
            for slot, at in pipeline(dve, tiles, 0):
                t = at(0)
                dve.wait_ge(product, t + 1)
                if had(t, RING):
                    dve.wait_ge(stored[slot], uses(t - RING, slot, 16))
                nc.vector.tensor_copy(y[:, slot, HALF:2 * HALF], ps[:, slot, HALF:2 * HALF]).then_inc(copied_v, 1)
            dve.wait_ge(counted, 1)
            nc.vector.tensor_scalar(k.windowed[:], ps_fits[:], float(P), None, ALU.is_equal).then_inc(flagged, 1)

        @block.gpsimd
        def _(pool):
            nc.gpsimd.iota(trash_i[:], pattern=[[0, 1]], base=TRASH, channel_multiplier=1).then_inc(trash_made, 1)
            nc.gpsimd.iota(iota_i[:], pattern=[[1, P]], base=0, channel_multiplier=0).then_inc(trash_made, 1)
            nc.gpsimd.memset(k.lower[:], 1.0).then_inc(ones, 1)
            pool.wait_ge(ones, 1)
            nc.gpsimd.affine_select(out=k.lower[:], in_=k.lower[:], compare_op=ALU.is_gt, fill=0.0, base=0,
                                    pattern=[[-1, P]], channel_multiplier=1).then_inc(made, 1)
            pool.wait_ge(zeroed, 1)
            n = 0
            for tables, width in ((k.sums0, C), (k.sums1, SW)):
                for table in tables:
                    per = ROWS * width // P
                    flat = table.rearrange("n w -> (n w)").rearrange("(p m) -> p m", p=P)
                    for a in range(0, per, 1024):
                        b = min(per, a + 1024)
                        nc.gpsimd.dma_start(flat[:, a:b], zeros[:, 0:b - a]).then_inc(zero_out, 16)
                        n += 1
            pool.wait_ge(zero_out, 16 * n)


def phase_weights(nc, k):
    with ExitStack() as ctx:
        sb = lambda n, s, d: ctx.enter_context(nc.sbuf_tensor(n, s, d))
        sem = lambda n: ctx.enter_context(nc.semaphore(n))
        mean = sb("w_mean", [P, G], FP32)
        rows = {"b1b": (k.b1b, C, True), "b2a": (k.b2a, H, True), "b2b": (k.b2b, C, False)}
        row = {n: sb(f"w_{n}", [1, w], FP32) for n, (_, w, _) in rows.items()}
        part = {n: sb(f"w_{n}_part", [1, 3, w], BF16) for n, (_, w, _) in rows.items()}
        rest = {n: sb(f"w_{n}_rest", [1, 2, w], FP32) for n, (_, w, _) in rows.items()}
        w_in, centred, split, rows_out = sem("w_in"), sem("w_centred"), sem("w_split"), sem("w_rows_out")
        zeroed, made = sem("w_zeroed"), sem("w_made")
        loads = [
            (k.w1a_x[:], k.W1a[0:C, :]), (k.w1a_e[:], k.W1a[C:2 * C, :]),
            (k.w1b_c[:], k.W1b.rearrange("(h p) n -> p h n", p=P)),
            (k.w2a_x[:], k.W2a[0:C, :]), (k.w2a_g[:], k.W2a[C:2 * C, :]),
            (k.w2b_c[:], k.W2b.rearrange("(h p) n -> p h n", p=P)),
            (k.gn1a[:, 0, :], k.g1a_w.rearrange("(h p) -> p h", p=P)), (k.gn1a[:, 1, :], k.g1a_b.rearrange("(h p) -> p h", p=P)),
            (k.gn2a[:, 0, :], k.g2a_w.rearrange("(h p) -> p h", p=P)), (k.gn2a[:, 1, :], k.g2a_b.rearrange("(h p) -> p h", p=P)),
            (k.b1a_all[:], k.b1a.partition_broadcast(P)), (k.bias0_all[:], k.bias0.partition_broadcast(P)),
        ] + [(d[:, j, :], s.partition_broadcast(P)) for d, s in ((k.g1b_w_all, k.g1b_w), (k.g1b_b_all, k.g1b_b)) for j in range(QT)] \
          + [(row[n][:], rows[n][0].unsqueeze(0)) for n in rows]
        block = ctx.enter_context(nc.Block())

        @block.sync
        def _(sp):
            with nc.allow_non_contiguous_dma("per-channel columns of the norms, once"):
                for to, source in loads:
                    sp.dma_start(to, source).then_inc(w_in, 16)
            sp.wait_ge(split, 5 * len(rows))
            for n, to in (("b1b", k.b1b_row), ("b2a", k.b2a_row), ("b2b", k.b2b_row)):
                for i in range(3):
                    sp.dma_start(to[i:i + 1, :], part[n][0:1, i, :]).then_inc(rows_out, 16)
            sp.wait_ge(rows_out, 16 * 3 * len(rows))

        @block.gpsimd
        def _(pool):
            identity(nc, pool, k.eye[:], zeroed, made)
            nc.gpsimd.memset(k.ones3[:], 1.0).then_inc(made, 1)
            nc.gpsimd.memset(k.eps[:], EPS).then_inc(made, 1)

        @block.vector
        def _(dve):
            dve.wait_ge(w_in, 16 * len(loads))
            at = 0
            both = [(k.w1a_x[:], P), (k.w1a_e[:], P), (k.w1b_c[:, 0, :], P), (k.w1b_c[:, 1, :], P), (k.w2a_x[:], P),
                    (k.w2a_g[:], P), (k.b1a_all[:], P)] + [(row[n][:], 1) for n in rows if rows[n][2]]
            for w, parts in both:
                v = w.rearrange("p (g k) -> p g k", g=G)
                m = mean[0:parts, :]
                nc.vector.tensor_reduce(m, v, AX.X, ALU.add).then_inc(centred, 1)
                dve.wait_ge(centred, at + 1)
                nc.vector.tensor_scalar(m, m, 1.0 / v.shape[2], None, ALU.mult).then_inc(centred, 1)
                dve.wait_ge(centred, at + 2)
                nc.vector.tensor_tensor(v, v, spread(m, parts, v.shape[2]), ALU.subtract).then_inc(centred, 1)
                dve.wait_ge(centred, at + 3)
                at += 3
            at = 0
            for n in rows:
                a, b, r, p3 = row[n][:], None, rest[n], part[n]
                nc.vector.tensor_copy(p3[:, 0, :], a).then_inc(split, 1)
                dve.wait_ge(split, at + 1)
                nc.vector.tensor_tensor(r[:, 0, :], a, p3[:, 0, :], ALU.subtract).then_inc(split, 1)
                dve.wait_ge(split, at + 2)
                nc.vector.tensor_copy(p3[:, 1, :], r[:, 0, :]).then_inc(split, 1)
                dve.wait_ge(split, at + 3)
                nc.vector.tensor_tensor(r[:, 1, :], r[:, 0, :], p3[:, 1, :], ALU.subtract).then_inc(split, 1)
                dve.wait_ge(split, at + 4)
                nc.vector.tensor_copy(p3[:, 2, :], r[:, 1, :]).then_inc(split, 1)
                at += 5


def compare_keys(nc, keys_row, key_f, q, eq, s):
    for j in range(QT):
        last = nc.vector.tensor_scalar(eq[:, j, :], keys_row[:, j * P:(j + 1) * P], key_f[:, bass.ds(q * QT + j, 1)],
                                       None, ALU.is_equal)
    last.then_inc(s, 1)


def first_of_key(nc, dve, q, lower, eq, before, key_f, key_trash, dup, mixed, idx, s_before, s_dup, s_mixed, s_idx):
    nc.vector.tensor_tensor(before, eq, lower.unsqueeze(1).broadcast_to((P, QT, P)), ALU.mult).then_inc(s_before, 1)
    dve.wait_ge(s_before, q + 1)
    nc.vector.tensor_reduce(dup, before, AX.X, ALU.max).then_inc(s_dup, 1)
    dve.wait_ge(s_dup, q + 1)
    nc.vector.tensor_tensor(mixed, dup, key_trash[:, bass.ds(q * QT, QT)], ALU.mult).then_inc(s_mixed, 1)
    dve.wait_ge(s_mixed, q + 1)
    nc.vector.tensor_tensor(idx, mixed, key_f[:, bass.ds(q * QT, QT)], ALU.add).then_inc(s_idx, 1)


def phase_edges0(nc, k):
    GATHER, KEYS, SCATTER = 0, 1, 2
    LAG = 2
    with ExitStack() as ctx:
        sb = lambda n, s, d: ctx.enter_context(nc.sbuf_tensor(n, s, d))
        sem = lambda n: ctx.enter_context(nc.semaphore(n))
        y_idx = sb("e0_y_idx", [P, RING, QT], I32)
        vals = sb("e0_vals", [P, RING, QT, C], FP32)
        keys = sb("e0_keys", [P, RING, QE], I32)
        eq = sb("e0_eq", [P, RING, QT, P], FP32)
        before = sb("e0_before", [P, QT, P], FP32)
        dup = sb("e0_dup", [P, QT], FP32)
        mixed = sb("e0_mixed", [P, QT], FP32)
        idx = sb("e0_idx", [P, RING, QT], I32)
        merged = sb("e0_merged", [P, RING, QT, C], FP32)
        ps = ctx.enter_context(nc.psum_tensor("e0_ps", [P, RING, QT, C], FP32))
        y_ready, eq_ready, before_ready, dup_ready, mixed_ready, idx_ready, sum_ready, out_ready = (
            sem(f"e0_{n}") for n in ("y_idx_ready", "eq_ready", "before", "dup", "mixed", "idx_ready", "sum_ready", "out_ready"))
        gathered = [sem(f"e0_gathered{i}") for i in range(RING)]
        keys_in = [sem(f"e0_keys_in{i}") for i in range(RING)]
        added = [sem(f"e0_added{i}") for i in range(K0)]
        issued = sem("e0_issued")
        block = ctx.enter_context(nc.Block())

        @block.sync
        def _(sp):
            for slot, at in pipeline(sp, Q, 0):
                q = at(0)
                if had(q, RING):
                    sp.wait_ge(eq_ready, q - 1)
                sp.dma_start(keys[:, slot, :], k.src_row[bass.ds(q * QE, QE)].partition_broadcast(P)).then_inc(keys_in[slot], 16)

        @block.gpsimd
        def _(pool):
            for slot, at in pipeline(pool, Q, LAG):
                if (q := at(GATHER)) is not None:
                    pool.wait_ge(y_ready, q + 1)
                    if had(q, RING):
                        pool.wait_ge(sum_ready, q - 1)
                    pool.sem_inc(issued, 1)
                    for j in range(QT):
                        nc.gpsimd.indirect_dma_start(vals[:, slot, j, :], None, k.y.rearrange("n (r c) -> (n r) c", r=R),
                                                     bass.IndirectOffsetOnAxis(ap=y_idx[:, slot, j:j + 1], axis=0)).then_inc(gathered[slot], 16)
                if (q := at(SCATTER)) is not None:
                    s = (slot + SCATTER) % RING
                    pool.wait_ge(out_ready, q + 1)
                    pool.wait_ge(idx_ready, q + 1)
                    if had(q, 1):
                        for j in range(QT):
                            pool.wait_ge(added[j], q * 16)
                    pool.sem_inc(issued, 1)
                    for j in range(QT):
                        nc.gpsimd.indirect_dma_start(k.sums0[j], bass.IndirectOffsetOnAxis(ap=idx[:, s, j:j + 1], axis=0),
                                                     merged[:, s, j, :], None, compute_op=ALU.add).then_inc(added[j], 16)
            for j in range(QT):
                pool.wait_ge(added[j], 16 * Q)

        @block.vector
        def _(dve):
            for slot, at in pipeline(dve, Q, LAG):
                if (q := at(GATHER)) is not None:
                    if had(q, RING):
                        dve.wait_ge(gathered[slot], uses(q - RING, slot, 16 * QT))
                    nc.vector.scalar_tensor_tensor(out=y_idx[:, slot, :], in0=k.dst_f[:, bass.ds(q * QT, QT)], scalar=float(R),
                                                   in1=k.type_i[:, bass.ds(q * QT, QT)], op0=ALU.mult, op1=ALU.add).then_inc(y_ready, 1)
                if (q := at(KEYS)) is not None:
                    s = (slot + KEYS) % RING
                    dve.wait_ge(keys_in[s], uses(q, s, 16))
                    if had(q, RING):
                        dve.wait_ge(sum_ready, q - 1)
                    compare_keys(nc, keys[:, s, :], k.src_f, q, eq[:, s], eq_ready)
                    dve.wait_ge(eq_ready, q + 1)
                    if had(q, RING):
                        for j in range(QT):
                            dve.wait_ge(added[j], q * 16 - 16)
                    first_of_key(nc, dve, q, k.lower[:], eq[:, s], before[:], k.src_f, k.src_trash, dup[:], mixed[:],
                                 idx[:, s, :], before_ready, dup_ready, mixed_ready, idx_ready)

        @block.tensor
        def _(pe):
            for slot, at in pipeline(pe, Q, 0):
                q = at(0)
                pe.wait_ge(gathered[slot], uses(q, slot, 16 * QT))
                pe.wait_ge(eq_ready, q + 1)
                if had(q, RING):
                    pe.wait_ge(out_ready, q - 1)
                for j in range(QT):
                    last = nc.tensor.matmul(ps[:, slot, j, :], eq[:, slot, j, :], vals[:, slot, j, :], start=True, stop=True)
                last.then_inc(sum_ready, 1)

        @block.scalar
        def _(act):
            for slot, at in pipeline(act, Q, 0):
                q = at(0)
                act.wait_ge(sum_ready, q + 1)
                if had(q, RING):
                    for j in range(QT):
                        act.wait_ge(added[j], q * 16 - 16)
                nc.scalar.copy(merged[:, slot].rearrange("p j c -> p (j c)"), ps[:, slot].rearrange("p j c -> p (j c)")).then_inc(out_ready, 1)


def node_rows(table, b):
    return table[bass.ds(b * BN, BN), :].rearrange("(p j) c -> p j c", j=NB)


class Chain:

    def __init__(self, eng, s, steps, b):
        self.eng, self.s, self.n = eng, s, b * steps

    def then(self, instruction):
        instruction.then_inc(self.s, 1)
        self.n = self.n + 1
        self.eng.wait_ge(self.s, self.n)


def phase_nodes1(nc, k):
    with ExitStack() as ctx:
        sb = lambda n, s, d: ctx.enter_context(nc.sbuf_tensor(n, s, d))
        sem = lambda n: ctx.enter_context(nc.semaphore(n))
        x = sb("n1_x", [P, RING, NB, C], FP32)
        sums = sb("n1_sums", [P, RING, K0, NB, C], FP32)
        h = sb("n1_h", [P, NB, C], FP32)
        sq = sb("n1_sq", [P, NB, C], FP32)
        x1 = sb("n1_x1", [P, RING, NB, C], FP32)
        xT = sb("n1_xT", [P, RING, NB, P], FP32)
        xa = sb("n1_xa", [P, RING, NB, H], FP32)
        mean, ss, sd, rs = (sb(f"n1_{n}", [P, NB], FP32) for n in ("mean", "ss", "sd", "rs"))
        psT = ctx.enter_context(nc.psum_tensor("n1_psT", [P, 2, 4, P], FP32))
        psA = ctx.enter_context(nc.psum_tensor("n1_psA", [P, 4, 2, H], FP32))
        step, centred, squared, var_ready, sd_ready, x1_ready, t_ready, xT_ready, xa_ready, xa_out = (
            sem(f"n1_{n}") for n in ("step", "centred", "squared", "var", "sd", "x1", "t", "xT", "xa", "xa_out"))
        x_in = [sem(f"n1_x_in{i}") for i in range(RING)]
        stored = [sem(f"n1_stored{i}") for i in range(RING)]
        STEPS = K0 + 1 + 2 + 1
        block = ctx.enter_context(nc.Block())

        @block.sync
        def _(sp):
            for slot, at in pipeline(sp, BLOCKS, 2):
                if (b := at(0)) is not None:
                    if had(b, RING):
                        sp.wait_ge(centred, b - 1)
                    sp.dma_start(x[:, slot], node_rows(k.x, b)).then_inc(x_in[slot], 16)
                    for c in range(K0):
                        sp.dma_start(sums[:, slot, c], node_rows(k.sums0[c], b)).then_inc(x_in[slot], 16)
                if (b := at(2)) is not None:
                    sp.wait_ge(x1_ready, b + 1)
                    sp.dma_start(node_rows(k.x1, b), x1[:, slot]).then_inc(stored[slot], 16)
                    sp.wait_ge(xT_ready, b + 1)
                    sp.dma_start(k.x1T[bass.ds(b, 1)].rearrange("a p m -> (a p) m"), xT[:, slot].rearrange("p j n -> p (j n)")).then_inc(stored[slot], 16)
                    sp.wait_ge(xa_out, b + 1)
                    sp.dma_start(node_rows(k.xa, b), xa[:, slot]).then_inc(stored[slot], 16)
            for slot in range(RING):
                sp.wait_ge(stored[slot], 48 * (BLOCKS // RING))

        @block.vector
        def _(dve):
            for slot, at in pipeline(dve, BLOCKS, 0):
                b = at(0)
                dve.wait_ge(x_in[slot], uses(b, slot, 16 * (K0 + 1)))
                if had(b, RING):
                    dve.wait_ge(stored[slot], uses(b - RING, slot, 48))
                chain = Chain(dve, step, STEPS, b)
                chain.then(nc.vector.tensor_tensor(h[:], x[:, slot], k.bias0_all[:].unsqueeze(1).broadcast_to((P, NB, C)), ALU.add))
                for c in range(K0):
                    chain.then(nc.vector.tensor_tensor(h[:], h[:], sums[:, slot, c], ALU.add))
                chain.then(nc.vector.tensor_reduce(mean[:], h[:], AX.X, ALU.add))
                chain.then(nc.vector.tensor_scalar(mean[:], mean[:], 1.0 / C, None, ALU.mult))
                nc.vector.tensor_tensor(h[:], h[:], spread(mean[:], P, C), ALU.subtract).then_inc(centred, 1)
                dve.wait_ge(squared, b + 1)
                nc.vector.tensor_reduce(ss[:], sq[:], AX.X, ALU.add).then_inc(var_ready, 1)
                dve.wait_ge(sd_ready, b + 1)
                chain.then(nc.vector.reciprocal(rs[:], sd[:]))
                if had(b, RING):
                    dve.wait_ge(t_ready, b - 1)
                nc.vector.tensor_tensor(x1[:, slot], h[:], spread(rs[:], P, C), ALU.mult).then_inc(x1_ready, 1)
                dve.wait_ge(xa_ready, b + 1)
                for i, n in ((0, 4), (1, NB - 4)):
                    out = nc.vector.tensor_tensor(xa[:, slot, 4 * i:4 * i + n], psA[:].rearrange("p a b h -> p (a b) h")[:, 4 * i:4 * i + n],
                                                  k.b1a_all[:].unsqueeze(1).broadcast_to((P, n, H)), ALU.add)
                out.then_inc(xa_out, 1)

        @block.scalar
        def _(act):
            for slot, at in pipeline(act, BLOCKS, 0):
                b = at(0)
                act.wait_ge(centred, b + 1)
                nc.scalar.activation(sq[:], h[:], ACT.Square).then_inc(squared, 1)
                act.wait_ge(var_ready, b + 1)
                nc.scalar.activation(sd[:], ss[:], ACT.Sqrt, bias=k.eps[:], scale=1.0 / C).then_inc(sd_ready, 1)
                act.wait_ge(t_ready, b + 1)
                if had(b, RING):
                    act.wait_ge(stored[slot], uses(b - RING, slot, 48))
                flat = psT[:].rearrange("p a b n -> p (a b) n")
                nc.scalar.copy(xT[:, slot], flat[:, 0:NB]).then_inc(xT_ready, 1)

        @block.tensor
        def _(pe):
            for slot, at in pipeline(pe, BLOCKS, 0):
                b = at(0)
                pe.wait_ge(x1_ready, b + 1)
                if had(b, 1):
                    pe.wait_ge(xT_ready, b)
                for j in range(NB):
                    last = nc.tensor.transpose(psT[:, j // 4, j % 4, :], x1[:, slot, j, :], k.eye[:])
                last.then_inc(t_ready, 1)
                pe.wait_ge(xT_ready, b + 1)
                if had(b, 1):
                    pe.wait_ge(xa_out, b)
                for j in range(NB):
                    last = nc.tensor.matmul(psA[:, j // 2, j % 2, :], xT[:, slot, j, :], k.w1a_x[:], start=True, stop=True)
                last.then_inc(xa_ready, 1)


def phase_edges1(nc, k):
    def either(eng, steps):
        windowed = eng.value_load(k.windowed[0:1, 0:1], min_val=0, max_val=1)
        with eng.If(windowed == 1):
            steps(eng, True)
        with eng.Else():
            steps(eng, False)

    LOAD, A, GN_A, T_B, GN_B, RELU_B, MERGE, SCATTER = 0, 2, 3, 4, 5, 5, 6, 7
    LAG = 8
    with ExitStack() as ctx:
        sb = lambda n, s, d: ctx.enter_context(nc.sbuf_tensor(n, s, d))
        sem = lambda n: ctx.enter_context(nc.semaphore(n))
        pb = lambda n, s: ctx.enter_context(nc.psum_tensor(n, s, FP32))
        ea = sb("e1_ea", [P, RING, QT, P], FP32)
        xa_idx = sb("e1_xa_idx", [P, RING, QT], I32)
        xa = sb("e1_xa", [P, RING, QT, H], FP32)
        sq_a = sb("e1_sq_a", [P, RING, QT * H], FP32)
        norm_a = sb("e1_norm_a", [P, RING, QT, H], FP32)
        hT = sb("e1_hT", [P, RING, 2, QT, P], FP32)
        sq_b = sb("e1_sq_b", [P, RING, QE], FP32)
        norm_b = sb("e1_norm_b", [P, RING, QE], FP32)
        h = sb("e1_h", [P, RING, QT, SW], FP32)
        ss_a, sd_a, rs_a, ss_b, sd_b, rs_b = (sb(f"e1_{n}", [P, RING, QT * G], FP32) for n in ("ss_a", "sd_a", "rs_a", "ss_b", "sd_b", "rs_b"))
        keys = sb("e1_keys", [P, RING, QE], I32)
        eq = sb("e1_eq", [P, RING, QT, P], FP32)
        before = sb("e1_before", [P, QT, P], FP32)
        dup = sb("e1_dup", [P, QT], FP32)
        mixed = sb("e1_mixed", [P, QT], FP32)
        idx = sb("e1_idx", [P, RING, QT], I32)
        merged = sb("e1_merged", [P, RING, QT, SW], FP32)
        window_sums = sb("e1_window_sums", [P, SW], FP32)
        psA, psT, psB, psM = pb("e1_psA", [P, RING, QT, H]), pb("e1_psT", [P, 2, QT, P]), pb("e1_psB", [P, QT, C]), pb("e1_psM", [P, QT * C])
        S = {n: sem(f"e1_{n}_ready") for n in ("xa_idx", "a", "sq_a", "ss_a", "sd_a", "rs_a", "norm_a", "t", "hT", "b", "sq_b", "ss_b", "sd_b", "rs_b", "norm_b",
                  "scaled", "shifted", "h", "eq", "before", "dup", "mixed", "idx", "counted", "sum", "out", "ones")}
        ea_in = [sem(f"e1_ea_in{i}") for i in range(RING)]
        keys_in = [sem(f"e1_keys_in{i}") for i in range(RING)]
        gathered = [sem(f"e1_gathered{i}") for i in range(RING)]
        added = [sem(f"e1_added{i}") for i in range(K1)]
        issued = sem("e1_issued")
        block = ctx.enter_context(nc.Block())
        at_slot = lambda slot, lag: (slot + lag) % RING

        def sync_steps(sp, windowed):
            for slot, at in pipeline(sp, Q, 4):
                if (q := at(LOAD)) is not None:
                    if had(q, RING):
                        sp.wait_ge(S["a"], q - 1)
                    sp.dma_start(ea[:, slot].rearrange("p j e -> p (j e)"), k.ea_T[:, bass.ds(q * QE, QE)]).then_inc(ea_in[slot], 16)
                if (q := at(4)) is not None and not windowed:
                    if had(q, RING):
                        sp.wait_ge(S["eq"], q - 1)
                    sp.dma_start(keys[:, slot, :], k.dst_row[bass.ds(q * QE, QE)].partition_broadcast(P)).then_inc(keys_in[slot], 16)

        def gpsimd_steps(pool, windowed):
            for slot, at in pipeline(pool, Q, LAG):
                if (q := at(LOAD)) is not None:
                    pool.wait_ge(S["xa_idx"], q + 1)
                    if had(q, RING):
                        pool.wait_ge(S["a"], q - 1)
                    pool.sem_inc(issued, 1)
                    for j in range(QT):
                        nc.gpsimd.indirect_dma_start(xa[:, slot, j, :], None, k.xa,
                                                     bass.IndirectOffsetOnAxis(ap=xa_idx[:, slot, j:j + 1], axis=0)).then_inc(gathered[slot], 16)
                q, s = at(SCATTER), at_slot(slot, SCATTER)
                if q is None:
                    continue
                if windowed and s == RING - 1:
                    w = at(SCATTER, RING)
                    pool.wait_ge(S["out"], w + 1)
                    if had(w, 1):
                        pool.wait_ge(added[0], w * 16)
                    pool.sem_inc(issued, 1)
                    first = pool.value_load(k.base_i[0:1, bass.ds(w, 1)], min_val=0, max_val=N)
                    nc.gpsimd.dma_start(k.sums1[0][bass.ds(first, P), :], window_sums[:], accum_op=ALU.add).then_inc(added[0], 16)
                if not windowed:
                    pool.wait_ge(S["out"], q + 1)
                    pool.wait_ge(S["counted"], q + 1)
                    pool.wait_ge(S["idx"], q + 1)
                    for j in range(QT):
                        if had(q, 1) or j >= K1:
                            pool.wait_ge(added[j % K1], q * (16 * QT // K1) + 16 * (j // K1))
                        pool.sem_inc(issued, 1)
                        nc.gpsimd.indirect_dma_start(k.sums1[j % K1], bass.IndirectOffsetOnAxis(ap=idx[:, s, j:j + 1], axis=0),
                                                     merged[:, s, j, :], None, compute_op=ALU.add).then_inc(added[j % K1], 16)
            if windowed:
                pool.wait_ge(added[0], 16 * W)
            else:
                for table in range(K1):
                    pool.wait_ge(added[table], 16 * QT // K1 * Q)

        def tensor_steps(pe, windowed):
            for slot, at in pipeline(pe, Q, 6):
                if (q := at(T_B)) is not None:
                    s = at_slot(slot, T_B)
                    pe.wait_ge(S["norm_a"], q + 1)
                    if had(q, 1):
                        pe.wait_ge(S["hT"], q)
                    for half in range(2):
                        for j in range(QT):
                            last = nc.tensor.transpose(psT[:, half, j, :], norm_a[:, s, j, half * P:(half + 1) * P], k.eye[:])
                    last.then_inc(S["t"], 1)
                if (q := at(MERGE)) is not None:
                    s = at_slot(slot, MERGE)
                    pe.wait_ge(S["h"], q + 1)
                    if isinstance(q, int) and q == 0:
                        pe.wait_ge(S["ones"], 1)
                    pe.wait_ge(S["eq"], q + 1)
                    if windowed:
                        w = at(MERGE, RING)
                        if s == 0 and had(w, 1):
                            pe.wait_ge(S["out"], w)
                        for j in range(QT):
                            last = nc.tensor.matmul(psM[:, 0:SW], eq[:, s, j, :], h[:, s, j, :], start=s == 0 and j == 0,
                                                    stop=s == RING - 1 and j == QT - 1)
                    else:
                        if had(q, 1):
                            pe.wait_ge(S["out"], q)
                        for j in range(QT):
                            last = nc.tensor.matmul(psM[:, j * C:(j + 1) * C], eq[:, s, j, :], h[:, s, j, 0:C], start=True, stop=True)
                    last.then_inc(S["sum"], 1)
                if (q := at(A)) is not None:
                    s = at_slot(slot, A)
                    pe.wait_ge(ea_in[s], uses(q, s, 16))
                    pe.wait_ge(gathered[s], uses(q, s, 16 * QT))
                    if had(q, RING):
                        pe.wait_ge(S["norm_a"], q - 1)
                    for j in range(QT):
                        nc.tensor.matmul(psA[:, s, j, :], ea[:, s, j, :], k.w1a_e[:], start=True, stop=False)
                        last = nc.tensor.matmul(psA[:, s, j, :], k.eye[:], xa[:, s, j, :], start=False, stop=True)
                    last.then_inc(S["a"], 1)
                if (q := at(T_B)) is not None:
                    s = at_slot(slot, T_B)
                    pe.wait_ge(S["hT"], q + 1)
                    if had(q, 1):
                        pe.wait_ge(S["norm_b"], q)
                    for j in range(QT):
                        nc.tensor.matmul(psB[:, j, :], k.ones3[:], k.b1b_row[:], start=True, stop=False)
                        nc.tensor.matmul(psB[:, j, :], hT[:, s, 0, j, :], k.w1b_c[:, 0, :], start=False, stop=False)
                        last = nc.tensor.matmul(psB[:, j, :], hT[:, s, 1, j, :], k.w1b_c[:, 1, :], start=False, stop=True)
                    last.then_inc(S["b"], 1)

        def scalar_steps(act, windowed):
            flat = lambda x: x.rearrange("p j c -> p (j c)")
            for slot, at in pipeline(act, Q, 6):
                if (q := at(GN_B)) is not None:
                    s = at_slot(slot, GN_B)
                    act.wait_ge(S["b"], q + 1)
                    if had(q, RING):
                        act.wait_ge(S["ss_b"], q - 1)
                    nc.scalar.activation(sq_b[:, s, :], flat(psB[:]), ACT.Square).then_inc(S["sq_b"], 1)
                if (q := at(T_B)) is not None:
                    s = at_slot(slot, T_B)
                    act.wait_ge(S["t"], q + 1)
                    if had(q, RING):
                        act.wait_ge(S["b"], q - 1)
                    for half in range(2):
                        last = nc.scalar.activation(flat(hT[:, s, half]), flat(psT[:, half]), ACT.Relu,
                                                    bias=k.gn1a[:, 1, half:half + 1], scale=k.gn1a[:, 0, half:half + 1])
                    last.then_inc(S["hT"], 1)
                if (q := at(GN_A)) is not None:
                    s = at_slot(slot, GN_A)
                    act.wait_ge(S["ss_a"], q + 1)
                    if had(q, RING):
                        act.wait_ge(S["rs_a"], q - 1)
                    nc.scalar.activation(sd_a[:, s, :], ss_a[:, s, :], ACT.Sqrt, bias=k.eps[:], scale=float(G) / H).then_inc(S["sd_a"], 1)
                if (q := at(GN_B)) is not None:
                    s = at_slot(slot, GN_B)
                    act.wait_ge(S["ss_b"], q + 1)
                    if had(q, RING):
                        act.wait_ge(S["rs_b"], q - 1)
                    nc.scalar.activation(sd_b[:, s, :], ss_b[:, s, :], ACT.Sqrt, bias=k.eps[:], scale=float(G) / C).then_inc(S["sd_b"], 1)
                if (q := at(A)) is not None:
                    s = at_slot(slot, A)
                    act.wait_ge(S["a"], q + 1)
                    if had(q, RING):
                        act.wait_ge(S["ss_a"], q - 1)
                    nc.scalar.activation(sq_a[:, s, :], flat(psA[:, s]), ACT.Square).then_inc(S["sq_a"], 1)
                if (q := at(RELU_B)) is not None:
                    s = at_slot(slot, RELU_B)
                    act.wait_ge(S["shifted"], q + 1)
                    if had(q, RING):
                        act.wait_ge(S["sum"], q - 1)
                    nc.scalar.activation(h[:, s, :, 0:C], norm_b[:, s, :].rearrange("p (j c) -> p j c", j=QT), ACT.Relu).then_inc(S["h"], 1)
                q, s = at(MERGE), at_slot(slot, MERGE)
                if q is not None and windowed and s == RING - 1:
                    w = at(MERGE, RING)
                    act.wait_ge(S["sum"], q + 1)
                    if had(w, 1):
                        act.wait_ge(added[0], w * 16)
                    nc.scalar.copy(window_sums[:], psM[:, 0:SW]).then_inc(S["out"], 1)
                if q is not None and not windowed:
                    act.wait_ge(S["sum"], q + 1)
                    if had(q, RING):
                        for table in range(K1):
                            act.wait_ge(added[table], q * (16 * QT // K1) - 16 * QT // K1)
                    nc.scalar.copy(merged[:, s, :, 0:C], psM[:].rearrange("p (j c) -> p j c", j=QT)).then_inc(S["out"], 1)

        def vector_steps(dve, windowed):
            groups = lambda x, n: x.rearrange("p (g k) -> p g k", g=n)
            nc.vector.memset(h[:, :, :, C:SW], 1.0).then_inc(S["ones"], 1)
            for slot, at in pipeline(dve, Q, 6):
                if (q := at(LOAD)) is not None:
                    if had(q, RING):
                        dve.wait_ge(gathered[slot], uses(q - RING, slot, 16 * QT))
                    nc.vector.tensor_copy(xa_idx[:, slot, :], k.src_idx[:, bass.ds(q * QT, QT)]).then_inc(S["xa_idx"], 1)
                if (q := at(GN_B)) is not None:
                    s = at_slot(slot, GN_B)
                    dve.wait_ge(S["sq_b"], q + 1)
                    if had(q, RING):
                        dve.wait_ge(S["sd_b"], q - 1)
                    nc.vector.tensor_reduce(ss_b[:, s, :], groups(sq_b[:, s, :], QT * G), AX.X, ALU.add).then_inc(S["ss_b"], 1)
                if (q := at(GN_A)) is not None:
                    s = at_slot(slot, GN_A)
                    dve.wait_ge(S["sq_a"], q + 1)
                    if had(q, RING):
                        dve.wait_ge(S["sd_a"], q - 1)
                    nc.vector.tensor_reduce(ss_a[:, s, :], groups(sq_a[:, s, :], QT * G), AX.X, ALU.add).then_inc(S["ss_a"], 1)
                if (q := at(GN_B)) is not None:
                    s = at_slot(slot, GN_B)
                    dve.wait_ge(S["sd_b"], q + 1)
                    nc.vector.reciprocal(rs_b[:, s, :], sd_b[:, s, :]).then_inc(S["rs_b"], 1)
                    dve.wait_ge(S["rs_b"], q + 1)
                    if had(q, RING):
                        dve.wait_ge(S["h"], q - 1)
                    nc.vector.tensor_tensor(groups(norm_b[:, s, :], QT * G), psB[:].rearrange("p j (g k) -> p (j g) k", g=G),
                                            spread(rs_b[:, s, :], P, C // G), ALU.mult).then_inc(S["norm_b"], 1)
                    dve.wait_ge(S["norm_b"], q + 1)
                    nc.vector.tensor_tensor(norm_b[:, s, :], norm_b[:, s, :], k.g1b_w_all[:].rearrange("p j c -> p (j c)"),
                                            ALU.mult).then_inc(S["scaled"], 1)
                    dve.wait_ge(S["scaled"], q + 1)
                    nc.vector.tensor_tensor(norm_b[:, s, :], norm_b[:, s, :], k.g1b_b_all[:].rearrange("p j c -> p (j c)"),
                                            ALU.add).then_inc(S["shifted"], 1)
                if (q := at(GN_A)) is not None:
                    s = at_slot(slot, GN_A)
                    dve.wait_ge(S["sd_a"], q + 1)
                    nc.vector.reciprocal(rs_a[:, s, :], sd_a[:, s, :]).then_inc(S["rs_a"], 1)
                    dve.wait_ge(S["rs_a"], q + 1)
                    if had(q, RING):
                        dve.wait_ge(S["t"], q - 1)
                    nc.vector.tensor_tensor(norm_a[:, s].rearrange("p j (g k) -> p (j g) k", g=G), psA[:, s].rearrange("p j (g k) -> p (j g) k", g=G),
                                            spread(rs_a[:, s, :], P, H // G), ALU.mult).then_inc(S["norm_a"], 1)
                if (q := at(GN_B)) is not None:
                    s = at_slot(slot, GN_B)
                    if had(q, RING):
                        dve.wait_ge(S["sum"], q - 1)
                    if windowed:
                        for j in range(QT):
                            last = nc.vector.tensor_scalar(eq[:, s, j, :], k.iota[:], k.rel[:, bass.ds(q * QT + j, 1)], None, ALU.is_equal)
                        last.then_inc(S["eq"], 1)
                        continue
                    dve.wait_ge(keys_in[s], uses(q, s, 16))
                    compare_keys(nc, keys[:, s, :], k.dst_f, q, eq[:, s], S["eq"])
                    dve.wait_ge(S["eq"], q + 1)
                    if had(q, RING):
                        for table in range(K1):
                            dve.wait_ge(added[table], q * (16 * QT // K1) - 16 * QT // K1)
                    nc.vector.tensor_reduce(merged[:, s, :, C:SW], eq[:, s], AX.X, ALU.add).then_inc(S["counted"], 1)
                    first_of_key(nc, dve, q, k.lower[:], eq[:, s], before[:], k.dst_f, k.dst_trash, dup[:], mixed[:],
                                 idx[:, s, :], S["before"], S["dup"], S["mixed"], S["idx"])

        @block.sync
        def _(sp):
            either(sp, sync_steps)

        @block.gpsimd
        def _(pool):
            either(pool, gpsimd_steps)

        @block.tensor
        def _(pe):
            either(pe, tensor_steps)

        @block.scalar
        def _(act):
            either(act, scalar_steps)

        @block.vector
        def _(dve):
            either(dve, vector_steps)


def phase_nodes2(nc, k):
    with ExitStack() as ctx:
        sb = lambda n, s, d: ctx.enter_context(nc.sbuf_tensor(n, s, d))
        sem = lambda n: ctx.enter_context(nc.semaphore(n))
        sums = sb("n2_sums", [P, RING, K1, NB, SW], FP32)
        x1 = sb("n2_x1", [P, RING, NB, C], FP32)
        xT = sb("n2_xT", [P, RING, NB, P], FP32)
        total = sb("n2_total", [P, NB, SW], FP32)
        agg = sb("n2_agg", [P, NB, C], FP32)
        aggT = sb("n2_aggT", [P, NB, P], FP32)
        sq = sb("n2_sq", [P, NB, H], FP32)
        norm = sb("n2_norm", [P, NB, H], FP32)
        hT = sb("n2_hT", [P, 2, NB, P], FP32)
        z = sb("n2_z", [P, NB, C], FP32)
        out = sb("n2_out", [P, RING, NB, C], FP32)
        cnt, mean, ss2, sd2, rs2 = (sb(f"n2_{n}", [P, NB], FP32) for n in ("cnt", "mean", "ss2", "sd2", "rs2"))
        ss, sd, rs = (sb(f"n2_{n}", [P, NB * G], FP32) for n in ("ss", "sd", "rs"))
        psT = ctx.enter_context(nc.psum_tensor("n2_psT", [P, 8, P], FP32))
        psU = ctx.enter_context(nc.psum_tensor("n2_psU", [P, 8, H], FP32))
        psH = psU[:].rearrange("p a (b n) -> p (a b) n", b=2)
        S = {n: sem(f"n2_{n}_ready") for n in ("step", "agg", "t", "aggT", "u", "sq", "ss", "sd", "norm", "th", "hT", "z", "centred", "sq2", "ss2", "sd2", "out")}
        loaded = [sem(f"n2_loaded{i}") for i in range(RING)]
        stored = [sem(f"n2_stored{i}") for i in range(RING)]
        STEPS = K1 - 1 + 2 + 1 + 1 + 2 + 1
        block = ctx.enter_context(nc.Block())

        @block.sync
        def _(sp):
            for slot, at in pipeline(sp, BLOCKS, 2):
                if (b := at(0)) is not None:
                    if had(b, RING):
                        sp.wait_ge(S["out"], b - 1)
                    for c in range(K1):
                        sp.dma_start(sums[:, slot, c], node_rows(k.sums1[c], b)).then_inc(loaded[slot], 16)
                    sp.dma_start(x1[:, slot], node_rows(k.x1, b)).then_inc(loaded[slot], 16)
                    sp.dma_start(xT[:, slot].rearrange("p j n -> p (j n)"), k.x1T[bass.ds(b, 1)].rearrange("a p m -> (a p) m")).then_inc(loaded[slot], 16)
                if (b := at(2)) is not None:
                    sp.wait_ge(S["out"], b + 1)
                    sp.dma_start(node_rows(k.out, b), out[:, slot]).then_inc(stored[slot], 16)
            for slot in range(RING):
                sp.wait_ge(stored[slot], 16 * (BLOCKS // RING))

        @block.vector
        def _(dve):
            for slot, at in pipeline(dve, BLOCKS, 0):
                b = at(0)
                dve.wait_ge(loaded[slot], uses(b, slot, 16 * (K1 + 2)))
                chain = Chain(dve, S["step"], STEPS, b)
                chain.then(nc.vector.tensor_tensor(total[:], sums[:, slot, 0], sums[:, slot, 1], ALU.add))
                for c in range(2, K1):
                    chain.then(nc.vector.tensor_tensor(total[:], total[:], sums[:, slot, c], ALU.add))
                chain.then(nc.vector.tensor_scalar(cnt[:], total[:, :, C], 1.0, None, ALU.max))
                chain.then(nc.vector.reciprocal(cnt[:], cnt[:]))
                if had(b, 1):
                    dve.wait_ge(S["t"], b)
                nc.vector.tensor_tensor(agg[:], total[:, :, 0:C], spread(cnt[:], P, C), ALU.mult).then_inc(S["agg"], 1)
                dve.wait_ge(S["sq"], b + 1)
                nc.vector.tensor_reduce(ss[:], sq[:].rearrange("p j (g k) -> p (j g) k", g=G), AX.X, ALU.add).then_inc(S["ss"], 1)
                dve.wait_ge(S["sd"], b + 1)
                chain.then(nc.vector.reciprocal(rs[:], sd[:]))
                nc.vector.tensor_tensor(norm[:].rearrange("p j (g k) -> p (j g) k", g=G), psU[:, 0:NB, :].rearrange("p j (g k) -> p (j g) k", g=G),
                                        spread(rs[:], P, H // G), ALU.mult).then_inc(S["norm"], 1)
                dve.wait_ge(S["z"], b + 1)
                chain.then(nc.vector.tensor_tensor(z[:], psT[:, 0:NB, :], x1[:, slot], ALU.add))
                chain.then(nc.vector.tensor_reduce(mean[:], z[:], AX.X, ALU.add))
                chain.then(nc.vector.tensor_scalar(mean[:], mean[:], 1.0 / C, None, ALU.mult))
                nc.vector.tensor_tensor(z[:], z[:], spread(mean[:], P, C), ALU.subtract).then_inc(S["centred"], 1)
                dve.wait_ge(S["sq2"], b + 1)
                nc.vector.tensor_reduce(ss2[:], sq[:, :, 0:C], AX.X, ALU.add).then_inc(S["ss2"], 1)
                dve.wait_ge(S["sd2"], b + 1)
                chain.then(nc.vector.reciprocal(rs2[:], sd2[:]))
                if had(b, RING):
                    dve.wait_ge(stored[slot], uses(b - RING, slot, 16))
                nc.vector.tensor_tensor(out[:, slot], z[:], spread(rs2[:], P, C), ALU.mult).then_inc(S["out"], 1)

        @block.scalar
        def _(act):
            for slot, at in pipeline(act, BLOCKS, 0):
                b = at(0)
                act.wait_ge(S["t"], b + 1)
                nc.scalar.copy(aggT[:], psT[:, 0:NB, :]).then_inc(S["aggT"], 1)
                act.wait_ge(S["u"], b + 1)
                nc.scalar.activation(sq[:], psU[:, 0:NB, :], ACT.Square).then_inc(S["sq"], 1)
                act.wait_ge(S["ss"], b + 1)
                nc.scalar.activation(sd[:], ss[:], ACT.Sqrt, bias=k.eps[:], scale=float(G) / H).then_inc(S["sd"], 1)
                act.wait_ge(S["th"], b + 1)
                for half in range(2):
                    last = nc.scalar.activation(hT[:, half], psH[:, half * 8:half * 8 + NB, :], ACT.Relu,
                                                bias=k.gn2a[:, 1, half:half + 1], scale=k.gn2a[:, 0, half:half + 1])
                last.then_inc(S["hT"], 1)
                act.wait_ge(S["centred"], b + 1)
                nc.scalar.activation(sq[:, :, 0:C], z[:], ACT.Square).then_inc(S["sq2"], 1)
                act.wait_ge(S["ss2"], b + 1)
                nc.scalar.activation(sd2[:], ss2[:], ACT.Sqrt, bias=k.eps[:], scale=1.0 / C).then_inc(S["sd2"], 1)

        @block.tensor
        def _(pe):
            for slot, at in pipeline(pe, BLOCKS, 0):
                b = at(0)
                pe.wait_ge(loaded[slot], uses(b, slot, 16 * (K1 + 2)))
                pe.wait_ge(S["agg"], b + 1)
                if had(b, 1):
                    pe.wait_ge(S["centred"], b)
                for j in range(NB):
                    last = nc.tensor.transpose(psT[:, j, :], agg[:, j, :], k.eye[:])
                last.then_inc(S["t"], 1)
                pe.wait_ge(S["aggT"], b + 1)
                for j in range(NB):
                    nc.tensor.matmul(psU[:, j, :], k.ones3[:], k.b2a_row[:], start=True, stop=False)
                    nc.tensor.matmul(psU[:, j, :], xT[:, slot, j, :], k.w2a_x[:], start=False, stop=False)
                    last = nc.tensor.matmul(psU[:, j, :], aggT[:, j, :], k.w2a_g[:], start=False, stop=True)
                last.then_inc(S["u"], 1)
                pe.wait_ge(S["norm"], b + 1)
                for half in range(2):
                    for j in range(NB):
                        last = nc.tensor.transpose(psH[:, half * 8 + j, :], norm[:, j, half * P:(half + 1) * P], k.eye[:])
                last.then_inc(S["th"], 1)
                pe.wait_ge(S["hT"], b + 1)
                for j in range(NB):
                    nc.tensor.matmul(psT[:, j, :], k.ones3[:], k.b2b_row[:], start=True, stop=False)
                    nc.tensor.matmul(psT[:, j, :], hT[:, 0, j, :], k.w2b_c[:, 0, :], start=False, stop=False)
                    last = nc.tensor.matmul(psT[:, j, :], hT[:, 1, j, :], k.w2b_c[:, 1, :], start=False, stop=True)
                last.then_inc(S["z"], 1)


def build(nc, k):
    k.y = nc.dram_tensor("y_table", (N, R * C), FP32, kind="Internal").ap()
    k.sums0 = [nc.dram_tensor(f"sums0_{c}", (ROWS, C), FP32, kind="Internal").ap() for c in range(K0)]
    k.sums1 = [nc.dram_tensor(f"sums1_{c}", (ROWS, SW), FP32, kind="Internal").ap() for c in range(K1)]
    k.xa = nc.dram_tensor("xa_table", (N, H), FP32, kind="Internal").ap()
    k.x1 = nc.dram_tensor("x1_table", (N, C), FP32, kind="Internal").ap()
    k.x1T = nc.dram_tensor("x1T_blocks", (BLOCKS, P, BN), FP32, kind="Internal").ap()
    with ExitStack() as ctx:
        sb = lambda n, s, d: ctx.enter_context(nc.sbuf_tensor(n, s, d))
        k.src_idx = sb("src_idx", [P, T], I32)
        k.type_i = sb("type_i", [P, T], I32)
        k.src_f = sb("src_f", [P, T], FP32)
        k.dst_f = sb("dst_f", [P, T], FP32)
        k.src_trash = sb("src_trash", [P, T], FP32)
        k.dst_trash = sb("dst_trash", [P, T], FP32)
        k.rel = sb("rel", [P, T], FP32)
        k.base_i = sb("base_i", [1, W], I32)
        k.windowed = sb("windowed", [1, 1], I32)
        k.iota = sb("iota", [P, P], FP32)
        k.lower = sb("lower", [P, P], FP32)
        k.eye = sb("eye", [P, P], FP32)
        k.eps = sb("eps", [P, 1], FP32)
        k.ones3 = sb("ones3", [3, P], BF16)
        k.w1a_x, k.w1a_e, k.w2a_x, k.w2a_g, k.b1a_all = (sb(n, [P, H], FP32) for n in ("w1a_x", "w1a_e", "w2a_x", "w2a_g", "b1a_all"))
        k.w1b_c, k.w2b_c = sb("w1b_c", [P, 2, C], FP32), sb("w2b_c", [P, 2, C], FP32)
        k.gn1a, k.gn2a = sb("gn1a", [P, 2, 2], FP32), sb("gn2a", [P, 2, 2], FP32)
        k.g1b_w_all, k.g1b_b_all = sb("g1b_w_all", [P, QT, C], FP32), sb("g1b_b_all", [P, QT, C], FP32)
        k.bias0_all = sb("bias0_all", [P, C], FP32)
        k.b1b_row, k.b2a_row, k.b2b_row = sb("b1b_row", [3, C], BF16), sb("b2a_row", [3, H], BF16), sb("b2b_row", [3, C], BF16)
        phase_tables(nc, k)
        phase_weights(nc, k)
        phase_edges0(nc, k)
        phase_nodes1(nc, k)
        phase_edges1(nc, k)
        phase_nodes2(nc, k)


def padded(a, rows, fill):
    return np.concatenate([a, np.full((rows - a.shape[0],) + a.shape[1:], fill, a.dtype)])


def kernel(**inputs):
    import concourse.bacc as bacc
    from concourse.bass_utils import run_bass_kernel_spmd

    a = {n: np.asarray(v) for n, v in inputs.items()}
    src, dst = (padded(a[n].astype(np.int32, copy=False), T * P, NODES) for n in ("src", "dst"))
    types = padded(a["edge_type_8"].astype(np.int32, copy=False), T * P, 0)
    x = padded(a["x"], N, 0)
    columns = lambda v: np.ascontiguousarray(v.reshape(T, P).T)
    arrays = {
        "x": x, "x_T": np.ascontiguousarray(x.T), "src_row": src, "dst_row": dst,
        "base_row": np.ascontiguousarray(dst[::WINDOW]), "src_cols": columns(src), "dst_cols": columns(dst), "type_cols": columns(types),
        "ea_T": np.ascontiguousarray(padded(a["edge_attr_128"], T * P, 0).T),
        "w_rel": np.ascontiguousarray(a["L0_gnn_weight"].transpose(1, 0, 2).reshape(C, R * C)),
        "bias0": a["L0_gnn_bias"], "W1a": a["L1_gnn_W1a"], "b1a": a["L1_gnn_b1a"], "W1b": a["L1_gnn_W1b"], "b1b": a["L1_gnn_b1b"],
        "W2a": a["L1_gnn_W2a"], "b2a": a["L1_gnn_b2a"], "W2b": a["L1_gnn_W2b"], "b2b": a["L1_gnn_b2b"],
        "g1a_w": a["L1_gnn_gn1a_w"], "g1a_b": a["L1_gnn_gn1a_b"], "g1b_w": a["L1_gnn_gn1b_w"], "g1b_b": a["L1_gnn_gn1b_b"],
        "g2a_w": a["L1_gnn_gn2a_w"], "g2a_b": a["L1_gnn_gn2a_b"],
    }
    nc = bacc.Bacc("TRN2", target_bir_lowering=False, num_devices=1)
    aps = {n: nc.dram_tensor(f"in_{n}", v.shape, mybir.dt.from_np(v.dtype), kind="ExternalInput").ap() for n, v in arrays.items()}
    k = Names()
    k.x, k.x_T, k.src_row, k.dst_row = (aps[n] for n in ("x", "x_T", "src_row", "dst_row"))
    k.src_cols, k.dst_cols, k.type_cols, k.ea_T = (aps[n] for n in ("src_cols", "dst_cols", "type_cols", "ea_T"))
    k.base_row = aps["base_row"]
    k.w_rel, k.bias0 = aps["w_rel"], aps["bias0"]
    k.W1a, k.b1a, k.W1b, k.b1b = (aps[n] for n in ("W1a", "b1a", "W1b", "b1b"))
    k.W2a, k.b2a, k.W2b, k.b2b = (aps[n] for n in ("W2a", "b2a", "W2b", "b2b"))
    k.g1a_w, k.g1a_b, k.g1b_w, k.g1b_b, k.g2a_w, k.g2a_b = (aps[n] for n in ("g1a_w", "g1a_b", "g1b_w", "g1b_b", "g2a_w", "g2a_b"))
    k.out = nc.dram_tensor("out", (N, C), FP32, kind="ExternalOutput").ap()
    build(nc, k)
    r = run_bass_kernel_spmd(nc, [{f"in_{n}": v for n, v in arrays.items()}], core_ids=[0])
    return r.results[0]["out"][0:NODES]
```

```python
from contextlib import ExitStack

import numpy as np
import concourse.bass as bass
from concourse import mybir

FP32, BF16, I32 = mybir.dt.float32, mybir.dt.bfloat16, mybir.dt.int32
ALU, ACT, AX = mybir.AluOpType, mybir.ActivationFunctionType, mybir.AxisListType

P = 128
C = 128
R = 8
H = 256
G = 8
NODES, EDGES = 12500, 212500
EPS = 1e-5
NB = 7
BLOCKS = 14
BN = NB * P
N = BN * BLOCKS
QT = 4
QE = QT * P
T = 1664
Q = T // QT
TRASH = N
ROWS = N + P
K0, K1 = 4, 2
WINDOW = 2 * QE
W = T * P // WINDOW
SW = C + 1
PE_ADDS = 2
RING = 2
TURN = 2 * RING
PICKED = 2
ZEROS = 2048
BANK = 512


class Names:
    pass


def pipeline(eng, count, lag, turn_steps=RING):
    head = -(-(lag + RING) // turn_steps) * turn_steps
    for s in range(head):
        yield s % turn_steps, lambda L, by=1: (s - L) // by if 0 <= s - L < count else None
    with eng.Fori(head // turn_steps, count // turn_steps) as turn:
        for u in range(turn_steps):
            yield u, lambda L, by=1: turn * (turn_steps // by) + (u - L) // by
    for s in range(count, count + lag):
        yield s % turn_steps, lambda L, by=1: (s - L) // by if 0 <= s - L < count else None


def quads(eng, lag):
    for step, at in pipeline(eng, Q, lag, TURN):
        yield step % RING, at


def had(q, n):
    return q - n >= 0 if isinstance(q, int) else True


def uses(q, slot, each):
    return (q - slot) * (each // RING) + each


def identity(nc, pool, eye, zeroed, made):
    nc.gpsimd.memset(eye, 0.0).then_inc(zeroed, 1)
    pool.wait_ge(zeroed, 1)
    nc.gpsimd.affine_select(out=eye, in_=eye, compare_op=ALU.not_equal, fill=1.0, base=0,
                            pattern=[[-1, P]], channel_multiplier=1).then_inc(made, 1)


def spread(per_group, parts, k):
    return per_group.unsqueeze(2).broadcast_to((parts, per_group.shape[1], k))


def zero_tables(eng, k, tables, width, out):
    n = 0
    for table in tables:
        per = ROWS * width // P
        flat = table.rearrange("n w -> (n w)").rearrange("(p m) -> p m", p=P)
        for a in range(0, per, ZEROS):
            b = min(per, a + ZEROS)
            eng.dma_start(flat[:, a:b], k.zeros[:, 0:b - a]).then_inc(out, 16)
            n += 1
    return n


def phase_tables(nc, k):
    HALF = R * C // 2
    with ExitStack() as ctx:
        sb = lambda n, s, d: ctx.enter_context(nc.sbuf_tensor(n, s, d))
        sem = lambda n: ctx.enter_context(nc.semaphore(n))
        w = sb("t_w", [P, R * C], FP32)
        xT = sb("t_xT", [P, RING, P], FP32)
        y = sb("t_y", [P, RING, R * C], FP32)
        dst_i = sb("t_dst_i", [P, T], I32)
        trash = sb("t_trash", [P, 1], FP32)
        trash_i = sb("t_trash_i", [P, 1], I32)
        base_i = sb("t_base_i", [P, W], I32)
        base_f = sb("t_base_f", [P, W], FP32)
        most, least, fits = sb("t_most", [P, 1], FP32), sb("t_least", [P, 1], FP32), sb("t_fits", [P, 1], FP32)
        ones_col = sb("t_ones_col", [P, 1], FP32)
        iota_i = sb("t_iota_i", [P, P], I32)
        iota_y_i = sb("t_iota_y_i", [P, R], I32)
        ps_fits = ctx.enter_context(nc.psum_tensor("t_ps_fits", [1, 1], FP32))
        ps = ctx.enter_context(nc.psum_tensor("t_ps", [P, RING, R * C], FP32))
        w_in, keys_in, zeroed, zero_out = sem("t_w_in"), sem("t_keys_in"), sem("t_zeroed"), sem("t_zero_out")
        x_in = [sem(f"t_x_in{i}") for i in range(RING)]
        product, copied_a, copied_v = sem("t_product"), sem("t_copied_act"), sem("t_copied_dve")
        stored = [sem(f"t_stored{i}") for i in range(RING)]
        cast, keyed, ones, made, trash_made = sem("t_cast"), sem("t_keyed"), sem("t_ones"), sem("t_made"), sem("t_trash")
        extremes, fit, counted, flagged = sem("t_extremes"), sem("t_fit"), sem("t_fit_counted"), sem("t_flagged")
        tiles = N // P
        block = ctx.enter_context(nc.Block())

        @block.sync
        def _(sp):
            sp.dma_start(w[:], k.w_rel).then_inc(w_in, 16)
            sp.dma_start(k.src_idx[:], k.src_cols).then_inc(keys_in, 16)
            sp.dma_start(dst_i[:], k.dst_cols).then_inc(keys_in, 16)
            sp.dma_start(k.type_i[:], k.type_cols).then_inc(keys_in, 16)
            sp.dma_start(base_i[:], k.base_row.partition_broadcast(P)).then_inc(keys_in, 16)
            sp.dma_start(k.base_i[:], k.base_row.unsqueeze(0)).then_inc(keys_in, 16)
            for slot, at in pipeline(sp, tiles, 2):
                if (t := at(0)) is not None:
                    if had(t, RING):
                        sp.wait_ge(product, t - 1)
                    sp.dma_start(xT[:, slot, :], k.x_T[:, bass.ds(t * P, P)]).then_inc(x_in[slot], 16)
                if (t := at(2)) is not None:
                    sp.wait_ge(copied_a, t + 1)
                    sp.wait_ge(copied_v, t + 1)
                    sp.dma_start(k.y[bass.ds(t * P, P), :], y[:, slot, :]).then_inc(stored[slot], 16)
            for slot in range(RING):
                sp.wait_ge(stored[slot], 16 * (tiles // RING))

        @block.tensor
        def _(pe):
            pe.wait_ge(w_in, 16)
            for slot, at in pipeline(pe, tiles, 0):
                t = at(0)
                pe.wait_ge(x_in[slot], uses(t, slot, 16))
                if had(t, RING):
                    pe.wait_ge(copied_a, t - 1)
                    pe.wait_ge(copied_v, t - 1)
                nc.tensor.matmul(ps[:, slot, 0:HALF], xT[:, slot, :], w[:, 0:HALF], start=True, stop=True)
                nc.tensor.matmul(ps[:, slot, HALF:2 * HALF], xT[:, slot, :], w[:, HALF:2 * HALF],
                                 start=True, stop=True).then_inc(product, 1)
            pe.wait_ge(fit, 2)
            nc.tensor.matmul(ps_fits[:], fits[:], ones_col[:], start=True, stop=True).then_inc(counted, 1)

        @block.scalar
        def _(act):
            for slot, at in pipeline(act, tiles, 0):
                t = at(0)
                act.wait_ge(product, t + 1)
                if had(t, RING):
                    act.wait_ge(stored[slot], uses(t - RING, slot, 16))
                nc.scalar.copy(y[:, slot, 0:HALF], ps[:, slot, 0:HALF]).then_inc(copied_a, 1)

        @block.vector
        def _(dve):
            nc.vector.memset(k.zeros[:], 0.0).then_inc(zeroed, 1)
            dve.wait_ge(keys_in, 80)
            dve.wait_ge(trash_made, 3)
            nc.vector.tensor_copy(k.src_f[:], k.src_idx[:]).then_inc(cast, 1)
            nc.vector.tensor_copy(k.dst_f[:], dst_i[:]).then_inc(cast, 1)
            nc.vector.tensor_copy(trash[:], trash_i[:]).then_inc(cast, 1)
            nc.vector.tensor_copy(base_f[:], base_i[:]).then_inc(cast, 1)
            nc.vector.tensor_copy(k.iota[:], iota_i[:]).then_inc(cast, 1)
            nc.vector.tensor_copy(k.iota_y[:], iota_y_i[:]).then_inc(cast, 1)
            nc.vector.memset(ones_col[:], 1.0).then_inc(cast, 1)
            dve.wait_ge(cast, 7)
            nc.vector.tensor_scalar(k.src_trash[:], k.src_f[:], -1.0, trash[:], ALU.mult, ALU.add).then_inc(keyed, 1)
            nc.vector.tensor_scalar(k.dst_trash[:], k.dst_f[:], -1.0, trash[:], ALU.mult, ALU.add).then_inc(keyed, 1)
            nc.vector.tensor_scalar(k.base_y[:], base_f[:], float(R), None, ALU.mult).then_inc(keyed, 1)
            nc.vector.tensor_tensor(k.rel[:].rearrange("p (w t) -> p w t", w=W), k.dst_f[:].rearrange("p (w t) -> p w t", w=W),
                                    spread(base_f[:], P, T // W), ALU.subtract).then_inc(keyed, 1)
            dve.wait_ge(keyed, 4)
            nc.vector.tensor_reduce(most[:], k.rel[:], AX.X, ALU.max).then_inc(extremes, 1)
            nc.vector.tensor_reduce(least[:], k.rel[:], AX.X, ALU.min).then_inc(extremes, 1)
            dve.wait_ge(extremes, 2)
            nc.vector.tensor_scalar(most[:], most[:], float(P - 1), None, ALU.is_le).then_inc(fit, 1)
            dve.wait_ge(fit, 1)
            nc.vector.scalar_tensor_tensor(out=fits[:], in0=least[:], scalar=0.0, in1=most[:], op0=ALU.is_ge, op1=ALU.mult).then_inc(fit, 1)
            for slot, at in pipeline(dve, tiles, 0):
                t = at(0)
                dve.wait_ge(product, t + 1)
                if had(t, RING):
                    dve.wait_ge(stored[slot], uses(t - RING, slot, 16))
                nc.vector.tensor_copy(y[:, slot, HALF:2 * HALF], ps[:, slot, HALF:2 * HALF]).then_inc(copied_v, 1)
            dve.wait_ge(counted, 1)
            nc.vector.tensor_scalar(k.windowed[:], ps_fits[:], float(P), None, ALU.is_equal).then_inc(flagged, 1)

        @block.gpsimd
        def _(pool):
            nc.gpsimd.iota(trash_i[:], pattern=[[0, 1]], base=TRASH, channel_multiplier=1).then_inc(trash_made, 1)
            nc.gpsimd.iota(iota_i[:], pattern=[[1, P]], base=0, channel_multiplier=0).then_inc(trash_made, 1)
            nc.gpsimd.iota(iota_y_i[:], pattern=[[1, R]], base=0, channel_multiplier=R).then_inc(trash_made, 1)
            nc.gpsimd.memset(k.lower[:], 1.0).then_inc(ones, 1)
            pool.wait_ge(ones, 1)
            nc.gpsimd.affine_select(out=k.lower[:], in_=k.lower[:], compare_op=ALU.is_gt, fill=0.0, base=0,
                                    pattern=[[-1, P]], channel_multiplier=1).then_inc(made, 1)
            pool.wait_ge(zeroed, 1)
            nc.gpsimd.dma_start(k.y[N:ROWS, :], k.zeros[:, 0:R * C]).then_inc(zero_out, 16)
            pool.wait_ge(zero_out, 16 + 16 * zero_tables(pool, k, k.sums0, C, zero_out))


def phase_weights(nc, k):
    with ExitStack() as ctx:
        sb = lambda n, s, d: ctx.enter_context(nc.sbuf_tensor(n, s, d))
        sem = lambda n: ctx.enter_context(nc.semaphore(n))
        mean = sb("w_mean", [P, G], FP32)
        rows = {"b1b": (k.b1b, C, True), "b2a": (k.b2a, H, True), "b2b": (k.b2b, C, False)}
        row = {n: sb(f"w_{n}", [1, w], FP32) for n, (_, w, _) in rows.items()}
        part = {n: sb(f"w_{n}_part", [1, 3, w], BF16) for n, (_, w, _) in rows.items()}
        rest = {n: sb(f"w_{n}_rest", [1, 2, w], FP32) for n, (_, w, _) in rows.items()}
        w_in, centred, split, rows_out = sem("w_in"), sem("w_centred"), sem("w_split"), sem("w_rows_out")
        zeroed, made = sem("w_zeroed"), sem("w_made")
        loads = [
            (k.w1a_x[:], k.W1a[0:C, :]), (k.w1a_e[:], k.W1a[C:2 * C, :]),
            (k.w1b_c[:], k.W1b.rearrange("(h p) n -> p h n", p=P)),
            (k.w2a_x[:], k.W2a[0:C, :]), (k.w2a_g[:], k.W2a[C:2 * C, :]),
            (k.w2b_c[:], k.W2b.rearrange("(h p) n -> p h n", p=P)),
            (k.gn1a[:, 0, :], k.g1a_w.rearrange("(h p) -> p h", p=P)), (k.gn1a[:, 1, :], k.g1a_b.rearrange("(h p) -> p h", p=P)),
            (k.gn2a[:, 0, :], k.g2a_w.rearrange("(h p) -> p h", p=P)), (k.gn2a[:, 1, :], k.g2a_b.rearrange("(h p) -> p h", p=P)),
            (k.b1a_all[:], k.b1a.partition_broadcast(P)), (k.bias0_all[:], k.bias0.partition_broadcast(P)),
        ] + [(d[:, j, :], s.partition_broadcast(P)) for d, s in ((k.g1b_w_all, k.g1b_w), (k.g1b_b_all, k.g1b_b)) for j in range(QT)] \
          + [(row[n][:], rows[n][0].unsqueeze(0)) for n in rows]
        block = ctx.enter_context(nc.Block())

        @block.sync
        def _(sp):
            with nc.allow_non_contiguous_dma("per-channel columns of the norms, once"):
                for to, source in loads:
                    sp.dma_start(to, source).then_inc(w_in, 16)
            sp.wait_ge(split, 5 * len(rows))
            copies = [(k.b1b_rows[:, j, :], "b1b") for j in range(QT)] + [(k.b2a_row[:], "b2a"), (k.b2b_row[:], "b2b")]
            for to, n in copies:
                for i in range(3):
                    sp.dma_start(to[i:i + 1, :], part[n][0:1, i, :]).then_inc(rows_out, 16)
            sp.wait_ge(rows_out, 16 * 3 * len(copies))

        @block.gpsimd
        def _(pool):
            identity(nc, pool, k.eye[:], zeroed, made)
            nc.gpsimd.memset(k.ones3[:], 1.0).then_inc(made, 1)
            nc.gpsimd.memset(k.eps[:], EPS).then_inc(made, 1)

        @block.vector
        def _(dve):
            dve.wait_ge(w_in, 16 * len(loads))
            at = 0
            both = [(k.w1a_x[:], P), (k.w1a_e[:], P), (k.w1b_c[:, 0, :], P), (k.w1b_c[:, 1, :], P), (k.w2a_x[:], P),
                    (k.w2a_g[:], P), (k.b1a_all[:], P)] + [(row[n][:], 1) for n in rows if rows[n][2]]
            for w, parts in both:
                v = w.rearrange("p (g k) -> p g k", g=G)
                m = mean[0:parts, :]
                nc.vector.tensor_reduce(m, v, AX.X, ALU.add).then_inc(centred, 1)
                dve.wait_ge(centred, at + 1)
                nc.vector.tensor_scalar(m, m, 1.0 / v.shape[2], None, ALU.mult).then_inc(centred, 1)
                dve.wait_ge(centred, at + 2)
                nc.vector.tensor_tensor(v, v, spread(m, parts, v.shape[2]), ALU.subtract).then_inc(centred, 1)
                dve.wait_ge(centred, at + 3)
                at += 3
            at = 0
            for n in rows:
                a, b, r, p3 = row[n][:], None, rest[n], part[n]
                nc.vector.tensor_copy(p3[:, 0, :], a).then_inc(split, 1)
                dve.wait_ge(split, at + 1)
                nc.vector.tensor_tensor(r[:, 0, :], a, p3[:, 0, :], ALU.subtract).then_inc(split, 1)
                dve.wait_ge(split, at + 2)
                nc.vector.tensor_copy(p3[:, 1, :], r[:, 0, :]).then_inc(split, 1)
                dve.wait_ge(split, at + 3)
                nc.vector.tensor_tensor(r[:, 1, :], r[:, 0, :], p3[:, 1, :], ALU.subtract).then_inc(split, 1)
                dve.wait_ge(split, at + 4)
                nc.vector.tensor_copy(p3[:, 2, :], r[:, 1, :]).then_inc(split, 1)
                at += 5


def compare_keys(nc, keys_row, key_f, q, eq, s):
    for j in range(QT):
        last = nc.vector.tensor_scalar(eq[:, j, :], keys_row[:, j * P:(j + 1) * P], key_f[:, bass.ds(q * QT + j, 1)],
                                       None, ALU.is_equal)
    last.then_inc(s, 1)


def first_of_key(nc, dve, q, lower, eq, before, key_f, key_trash, dup, mixed, idx, s_before, s_dup, s_mixed, s_idx):
    nc.vector.tensor_tensor(before, eq, lower.unsqueeze(1).broadcast_to((P, QT, P)), ALU.mult).then_inc(s_before, 1)
    dve.wait_ge(s_before, q + 1)
    nc.vector.tensor_reduce(dup, before, AX.X, ALU.max).then_inc(s_dup, 1)
    dve.wait_ge(s_dup, q + 1)
    nc.vector.tensor_tensor(mixed, dup, key_trash[:, bass.ds(q * QT, QT)], ALU.mult).then_inc(s_mixed, 1)
    dve.wait_ge(s_mixed, q + 1)
    nc.vector.tensor_tensor(idx, mixed, key_f[:, bass.ds(q * QT, QT)], ALU.add).then_inc(s_idx, 1)


def either(k, eng, steps):
    windowed = eng.value_load(k.windowed[0:1, 0:1], min_val=0, max_val=1)
    with eng.If(windowed == 1):
        steps(eng, True)
    with eng.Else():
        steps(eng, False)


def phase_edges0(nc, k):
    LOAD, GATHER, MATCH, PICK, KEYS, MERGE, SCATTER = 0, 1, 1, 2, 2, 3, 3
    with ExitStack() as ctx:
        sb = lambda n, s, d: ctx.enter_context(nc.sbuf_tensor(n, s, d))
        sem = lambda n: ctx.enter_context(nc.semaphore(n))
        y_idx = sb("e0_y_idx", [P, RING, QT], I32)
        vals = sb("e0_vals", [P, RING, QT, C], FP32)
        keys = sb("e0_keys", [P, RING, QE], I32)
        dst_keys = sb("e0_dst_keys", [P, RING, PICKED * P], I32)
        type_keys = sb("e0_type_keys", [P, RING, PICKED * P], I32)
        y_keys = sb("e0_y_keys", [P, PICKED * P], FP32)
        y_rows = sb("e0_y_rows", [P, R], FP32)
        picks = sb("e0_picks", [P, RING, R, PICKED * P], FP32)
        y_window = sb("e0_y_window", [P, 2, R * C], FP32)
        eq = sb("e0_eq", [P, RING, QT, P], FP32)
        before = sb("e0_before", [P, QT, P], FP32)
        dup = sb("e0_dup", [P, QT], FP32)
        mixed = sb("e0_mixed", [P, QT], FP32)
        idx = sb("e0_idx", [P, RING, QT], I32)
        merged = sb("e0_merged", [P, RING, QT, C], FP32)
        ps = ctx.enter_context(nc.psum_tensor("e0_ps", [P, RING, QT, C], FP32))
        ps_picked = ctx.enter_context(nc.psum_tensor("e0_ps_picked", [P, RING, BANK], FP32))
        y_ready, y_keys_ready, y_rows_ready, picks_ready, product_ready, picked_ready, eq_ready, before_ready, dup_ready, mixed_ready, idx_ready, sum_ready, out_ready = (
            sem(f"e0_{n}") for n in ("y_idx_ready", "y_keys", "y_rows", "picks", "product", "picked", "eq_ready", "before", "dup", "mixed", "idx_ready",
                                     "sum_ready", "out_ready"))
        gathered = [sem(f"e0_gathered{i}") for i in range(RING)]
        keys_in = [sem(f"e0_keys_in{i}") for i in range(RING)]
        y_keys_in = [sem(f"e0_y_keys_in{i}") for i in range(RING)]
        window_in = [sem(f"e0_window_in{i}") for i in range(2)]
        added = [sem(f"e0_added{i}") for i in range(K0)]
        zero_out = sem("e0_zero_out")
        issued = sem("e0_issued")
        block = ctx.enter_context(nc.Block())
        at_slot = lambda slot, lag: (slot + lag) % RING
        first_gathered = lambda windowed: PICKED if windowed else 0

        def sync_steps(sp, windowed):
            for step, at in pipeline(sp, Q, 0, TURN):
                q, slot = at(LOAD), step % RING
                if windowed:
                    for to, source in ((dst_keys, k.dst_row), (type_keys, k.type_row)):
                        if had(q, RING):
                            sp.wait_ge(y_keys_ready, q - 1)
                        sp.dma_start(to[:, slot, :], source[bass.ds(q * QE, PICKED * P)].partition_broadcast(P)).then_inc(y_keys_in[slot], 16)
                if windowed and slot == 0:
                    w, half = at(LOAD, RING), step // RING
                    if had(w, 2):
                        sp.wait_ge(product_ready, q - RING)
                    first = sp.value_load(k.base_i[0:1, bass.ds(w, 1)], min_val=0, max_val=N)
                    sp.dma_start(y_window[:, half, :], k.y[bass.ds(first, P), :]).then_inc(window_in[half], 16)
                if had(q, RING):
                    sp.wait_ge(eq_ready, q - 1)
                sp.dma_start(keys[:, slot, :], k.src_row[bass.ds(q * QE, QE)].partition_broadcast(P)).then_inc(keys_in[slot], 16)

        def gpsimd_steps(pool, windowed):
            start = first_gathered(windowed)
            for slot, at in quads(pool, SCATTER):
                if (q := at(GATHER)) is not None:
                    s = at_slot(slot, GATHER)
                    pool.wait_ge(y_ready, q + 1)
                    if had(q, RING):
                        pool.wait_ge(sum_ready, q - 1)
                    pool.sem_inc(issued, 1)
                    for j in range(start, QT):
                        nc.gpsimd.indirect_dma_start(vals[:, s, j, :], None, k.y.rearrange("n (r c) -> (n r) c", r=R),
                                                     bass.IndirectOffsetOnAxis(ap=y_idx[:, s, j:j + 1], axis=0)).then_inc(gathered[s], 16)
                if (q := at(SCATTER)) is not None:
                    s = at_slot(slot, SCATTER)
                    pool.wait_ge(out_ready, q + 1)
                    pool.wait_ge(idx_ready, q + 1)
                    if had(q, 1):
                        for j in range(QT):
                            pool.wait_ge(added[j], q * 16)
                    pool.sem_inc(issued, 1)
                    for j in range(QT):
                        nc.gpsimd.indirect_dma_start(k.sums0[j], bass.IndirectOffsetOnAxis(ap=idx[:, s, j:j + 1], axis=0),
                                                     merged[:, s, j, :], None, compute_op=ALU.add).then_inc(added[j], 16)
            for j in range(QT):
                pool.wait_ge(added[j], 16 * Q)

        def vector_steps(dve, windowed):
            each = 16 * (QT - first_gathered(windowed))
            for slot, at in quads(dve, KEYS):
                if (q := at(GATHER)) is not None:
                    s = at_slot(slot, GATHER)
                    if had(q, RING):
                        dve.wait_ge(gathered[s], uses(q - RING, s, each))
                    nc.vector.scalar_tensor_tensor(out=y_idx[:, s, :], in0=k.dst_f[:, bass.ds(q * QT, QT)], scalar=float(R),
                                                   in1=k.type_i[:, bass.ds(q * QT, QT)], op0=ALU.mult, op1=ALU.add).then_inc(y_ready, 1)
                if (q := at(MATCH)) is not None and windowed:
                    s = at_slot(slot, MATCH)
                    dve.wait_ge(y_keys_in[s], uses(q, s, 32))
                    if had(q, 1):
                        dve.wait_ge(picks_ready, q)
                    nc.vector.scalar_tensor_tensor(out=y_keys[:], in0=dst_keys[:, s, :], scalar=float(R), in1=type_keys[:, s, :],
                                                   op0=ALU.mult, op1=ALU.add).then_inc(y_keys_ready, 1)
                    nc.vector.tensor_scalar(y_rows[:], k.iota_y[:], k.base_y[:, bass.ds(at(MATCH, RING), 1)], None, ALU.add).then_inc(y_rows_ready, 1)
                    dve.wait_ge(y_keys_ready, q + 1)
                    dve.wait_ge(y_rows_ready, q + 1)
                    if had(q, RING):
                        dve.wait_ge(product_ready, q - 1)
                    nc.vector.tensor_tensor(picks[:, s], y_keys[:].unsqueeze(1).broadcast_to((P, R, PICKED * P)), spread(y_rows[:], P, PICKED * P),
                                            ALU.is_equal).then_inc(picks_ready, 1)
                if (q := at(KEYS)) is not None:
                    s = at_slot(slot, KEYS)
                    dve.wait_ge(keys_in[s], uses(q, s, 16))
                    if had(q, RING):
                        dve.wait_ge(sum_ready, q - 1)
                    compare_keys(nc, keys[:, s, :], k.src_f, q, eq[:, s], eq_ready)
                    dve.wait_ge(eq_ready, q + 1)
                    if had(q, RING):
                        for j in range(QT):
                            dve.wait_ge(added[j], q * 16 - 16)
                    first_of_key(nc, dve, q, k.lower[:], eq[:, s], before[:], k.src_f, k.src_trash, dup[:], mixed[:],
                                 idx[:, s, :], before_ready, dup_ready, mixed_ready, idx_ready)

        def tensor_steps(pe, windowed):
            for step, at in pipeline(pe, Q, MERGE, TURN):
                if (q := at(MERGE)) is not None:
                    s = at_slot(step, MERGE)
                    if windowed:
                        pe.wait_ge(picked_ready, q + 1)
                    pe.wait_ge(gathered[s], uses(q, s, 16 * (QT - first_gathered(windowed))))
                    pe.wait_ge(eq_ready, q + 1)
                    if had(q, RING):
                        pe.wait_ge(out_ready, q - 1)
                    for j in range(QT):
                        last = nc.tensor.matmul(ps[:, s, j, :], eq[:, s, j, :], vals[:, s, j, :], start=True, stop=True)
                    last.then_inc(sum_ready, 1)
                if (q := at(PICK)) is not None and windowed:
                    s = at_slot(step, PICK)
                    half = (step - PICK) % TURN // RING
                    pe.wait_ge(picks_ready, q + 1)
                    pe.wait_ge(window_in[half], uses(at(PICK, RING), half, 16))
                    if had(q, RING):
                        pe.wait_ge(picked_ready, q - 1)
                    for j in range(PICKED):
                        for r in range(R):
                            last = nc.tensor.matmul(ps_picked[:, s, j * C:(j + 1) * C], picks[:, s, r, j * P:(j + 1) * P],
                                                    y_window[:, half, r * C:(r + 1) * C], start=r == 0, stop=r == R - 1)
                    last.then_inc(product_ready, 1)

        def scalar_steps(act, windowed):
            for slot, at in quads(act, MERGE):
                if (q := at(MERGE)) is not None:
                    s = at_slot(slot, MERGE)
                    act.wait_ge(sum_ready, q + 1)
                    if had(q, RING):
                        for j in range(QT):
                            act.wait_ge(added[j], q * 16 - 16)
                    nc.scalar.copy(merged[:, s].rearrange("p j c -> p (j c)"), ps[:, s].rearrange("p j c -> p (j c)")).then_inc(out_ready, 1)
                if (q := at(PICK)) is not None and windowed:
                    s = at_slot(slot, PICK)
                    act.wait_ge(product_ready, q + 1)
                    if had(q, RING):
                        act.wait_ge(sum_ready, q - 1)
                    nc.scalar.copy(vals[:, s, 0:PICKED].rearrange("p j c -> p (j c)"), ps_picked[:, s, 0:PICKED * C]).then_inc(picked_ready, 1)

        @block.sync
        def _(sp):
            either(k, sp, sync_steps)

        @block.gpsimd
        def _(pool):
            either(k, pool, gpsimd_steps)

        @block.tensor
        def _(pe):
            either(k, pe, tensor_steps)

        @block.scalar
        def _(act):
            zeroing = zero_tables(act, k, k.sums1, SW, zero_out)
            either(k, act, scalar_steps)
            act.wait_ge(zero_out, 16 * zeroing)

        @block.vector
        def _(dve):
            either(k, dve, vector_steps)


def node_rows(table, b):
    return table[bass.ds(b * BN, BN), :].rearrange("(p j) c -> p j c", j=NB)


class Chain:

    def __init__(self, eng, s, steps, b):
        self.eng, self.s, self.n = eng, s, b * steps

    def then(self, instruction):
        instruction.then_inc(self.s, 1)
        self.n = self.n + 1
        self.eng.wait_ge(self.s, self.n)


def phase_nodes1(nc, k):
    LOAD, SUM, NORM, XA, STORE = 0, 1, 2, 3, 4
    with ExitStack() as ctx:
        sb = lambda n, s, d: ctx.enter_context(nc.sbuf_tensor(n, s, d))
        sem = lambda n: ctx.enter_context(nc.semaphore(n))
        x = sb("n1_x", [P, RING, NB, C], FP32)
        sums = sb("n1_sums", [P, RING, K0, NB, C], FP32)
        h = sb("n1_h", [P, NB, C], FP32)
        sq = sb("n1_sq", [P, NB, C], FP32)
        x1 = sb("n1_x1", [P, RING, NB, C], FP32)
        xT = sb("n1_xT", [P, RING, NB, P], FP32)
        xa = sb("n1_xa", [P, RING, NB, H], FP32)
        mean, ss, sd, rs = (sb(f"n1_{n}", [P, NB], FP32) for n in ("mean", "ss", "sd", "rs"))
        psT = ctx.enter_context(nc.psum_tensor("n1_psT", [P, 2, 4, P], FP32))
        psA = ctx.enter_context(nc.psum_tensor("n1_psA", [P, 4, 2, H], FP32))
        summed, reciprocals, centred, squared, var_ready, sd_ready, x1_ready, t_ready, xT_ready, xa_ready, xa_out = (
            sem(f"n1_{n}") for n in ("summed", "reciprocals", "centred", "squared", "var", "sd", "x1", "t", "xT", "xa", "xa_out"))
        x_in = [sem(f"n1_x_in{i}") for i in range(RING)]
        stored = [sem(f"n1_stored{i}") for i in range(RING)]
        xa_stored = [sem(f"n1_xa_stored{i}") for i in range(RING)]
        block = ctx.enter_context(nc.Block())
        at_slot = lambda slot, lag: (slot + lag) % RING

        @block.sync
        def _(sp):
            for slot, at in pipeline(sp, BLOCKS, STORE):
                if (b := at(LOAD)) is not None:
                    if had(b, RING):
                        sp.wait_ge(centred, b - 1)
                    sp.dma_start(x[:, slot], node_rows(k.x, b)).then_inc(x_in[slot], 16)
                    for c in range(K0):
                        sp.dma_start(sums[:, slot, c], node_rows(k.sums0[c], b)).then_inc(x_in[slot], 16)
                if (b := at(XA)) is not None:
                    s = at_slot(slot, XA)
                    sp.wait_ge(x1_ready, b + 1)
                    sp.dma_start(node_rows(k.x1, b), x1[:, s]).then_inc(stored[s], 16)
                    sp.wait_ge(xT_ready, b + 1)
                    sp.dma_start(k.x1T[bass.ds(b, 1)].rearrange("a p m -> (a p) m"), xT[:, s].rearrange("p j n -> p (j n)")).then_inc(stored[s], 16)
                if (b := at(STORE)) is not None:
                    s = at_slot(slot, STORE)
                    sp.wait_ge(xa_out, b + 1)
                    sp.dma_start(node_rows(k.xa, b), xa[:, s]).then_inc(xa_stored[s], 16)
            for slot in range(RING):
                sp.wait_ge(stored[slot], 32 * (BLOCKS // RING))
                sp.wait_ge(xa_stored[slot], 16 * (BLOCKS // RING))

        @block.vector
        def _(dve):
            for slot, at in pipeline(dve, BLOCKS, XA):
                if (b := at(XA)) is not None:
                    s = at_slot(slot, XA)
                    dve.wait_ge(xa_ready, b + 1)
                    if had(b, RING):
                        dve.wait_ge(xa_stored[s], uses(b - RING, s, 16))
                    for i, n in ((0, 4), (1, NB - 4)):
                        out = nc.vector.tensor_tensor(xa[:, s, 4 * i:4 * i + n], psA[:].rearrange("p a b h -> p (a b) h")[:, 4 * i:4 * i + n],
                                                      k.b1a_all[:].unsqueeze(1).broadcast_to((P, n, H)), ALU.add)
                    out.then_inc(xa_out, 1)
                if (b := at(NORM)) is not None:
                    s = at_slot(slot, NORM)
                    dve.wait_ge(squared, b + 1)
                    nc.vector.tensor_reduce(ss[:], sq[:], AX.X, ALU.add).then_inc(var_ready, 1)
                    dve.wait_ge(sd_ready, b + 1)
                    nc.vector.reciprocal(rs[:], sd[:]).then_inc(reciprocals, 1)
                    dve.wait_ge(reciprocals, b + 1)
                    if had(b, RING):
                        dve.wait_ge(t_ready, b - 1)
                        dve.wait_ge(stored[s], uses(b - RING, s, 32))
                    nc.vector.tensor_tensor(x1[:, s], h[:], spread(rs[:], P, C), ALU.mult).then_inc(x1_ready, 1)
                if (b := at(SUM)) is not None:
                    s = at_slot(slot, SUM)
                    dve.wait_ge(x_in[s], uses(b, s, 16 * (K0 + 1)))
                    if had(b, 1):
                        dve.wait_ge(x1_ready, b)
                    chain = Chain(dve, summed, 1 + K0 + 2, b)
                    chain.then(nc.vector.tensor_tensor(h[:], x[:, s], k.bias0_all[:].unsqueeze(1).broadcast_to((P, NB, C)), ALU.add))
                    for c in range(K0):
                        chain.then(nc.vector.tensor_tensor(h[:], h[:], sums[:, s, c], ALU.add))
                    chain.then(nc.vector.tensor_reduce(mean[:], h[:], AX.X, ALU.add))
                    chain.then(nc.vector.tensor_scalar(mean[:], mean[:], 1.0 / C, None, ALU.mult))
                    nc.vector.tensor_tensor(h[:], h[:], spread(mean[:], P, C), ALU.subtract).then_inc(centred, 1)

        @block.scalar
        def _(act):
            for slot, at in pipeline(act, BLOCKS, NORM):
                if (b := at(NORM)) is not None:
                    s = at_slot(slot, NORM)
                    act.wait_ge(var_ready, b + 1)
                    nc.scalar.activation(sd[:], ss[:], ACT.Sqrt, bias=k.eps[:], scale=1.0 / C).then_inc(sd_ready, 1)
                    act.wait_ge(t_ready, b + 1)
                    if had(b, RING):
                        act.wait_ge(stored[s], uses(b - RING, s, 32))
                        act.wait_ge(xa_ready, b - 1)
                    flat = psT[:].rearrange("p a b n -> p (a b) n")
                    nc.scalar.copy(xT[:, s], flat[:, 0:NB]).then_inc(xT_ready, 1)
                if (b := at(SUM)) is not None:
                    act.wait_ge(centred, b + 1)
                    nc.scalar.activation(sq[:], h[:], ACT.Square).then_inc(squared, 1)

        @block.tensor
        def _(pe):
            for slot, at in pipeline(pe, BLOCKS, 0):
                b = at(0)
                pe.wait_ge(x1_ready, b + 1)
                if had(b, 1):
                    pe.wait_ge(xT_ready, b)
                for j in range(NB):
                    last = nc.tensor.transpose(psT[:, j // 4, j % 4, :], x1[:, slot, j, :], k.eye[:])
                last.then_inc(t_ready, 1)
                pe.wait_ge(xT_ready, b + 1)
                if had(b, 1):
                    pe.wait_ge(xa_out, b)
                for j in range(NB):
                    last = nc.tensor.matmul(psA[:, j // 2, j % 2, :], xT[:, slot, j, :], k.w1a_x[:], start=True, stop=True)
                last.then_inc(xa_ready, 1)


def phase_edges1(nc, k):
    LOAD, GATHER, A, ADD, GN_A, TURN, B, GN_B, SCALE, SHIFT, EQ, RELU_B, MERGE, SCATTER = 0, 0, 2, 2, 3, 4, 5, 5, 6, 7, 7, 7, 8, 9
    LAG = 9
    with ExitStack() as ctx:
        sb = lambda n, s, d: ctx.enter_context(nc.sbuf_tensor(n, s, d))
        sem = lambda n: ctx.enter_context(nc.semaphore(n))
        pb = lambda n, s: ctx.enter_context(nc.psum_tensor(n, s, FP32))
        ea = sb("e1_ea", [P, RING, QT, P], FP32)
        xa_idx = sb("e1_xa_idx", [P, RING, QT], I32)
        xa = sb("e1_xa", [P, RING, QT, H], FP32)
        shifted_b = sb("e1_shifted_b", [P, RING, QE], FP32)
        sq_a = sb("e1_sq_a", [P, RING, QT * H], FP32)
        norm_a = sb("e1_norm_a", [P, RING, QT, H], FP32)
        hT = sb("e1_hT", [P, RING, 2, QT, P], FP32)
        sq_b = sb("e1_sq_b", [P, RING, QE], FP32)
        norm_b = sb("e1_norm_b", [P, RING, QE], FP32)
        h = sb("e1_h", [P, RING, QT, SW], FP32)
        ss_a, sd_a, rs_a, ss_b, sd_b, rs_b = (sb(f"e1_{n}", [P, RING, QT * G], FP32) for n in ("ss_a", "sd_a", "rs_a", "ss_b", "sd_b", "rs_b"))
        keys = sb("e1_keys", [P, RING, QE], I32)
        eq = sb("e1_eq", [P, RING, QT, P], FP32)
        before = sb("e1_before", [P, QT, P], FP32)
        dup = sb("e1_dup", [P, QT], FP32)
        mixed = sb("e1_mixed", [P, QT], FP32)
        idx = sb("e1_idx", [P, RING, QT], I32)
        merged = sb("e1_merged", [P, RING, QT, SW], FP32)
        window_sums = sb("e1_window_sums", [P, SW], FP32)
        psA, psT, psB, psM = pb("e1_psA", [P, RING, QT, H]), pb("e1_psT", [P, 2, QT, P]), pb("e1_psB", [P, QT, C]), pb("e1_psM", [P, QT * C])
        S = {n: sem(f"e1_{n}_ready") for n in ("xa_idx", "a_edge", "a", "sum_a", "sq_a", "ss_a", "sd_a", "rs_a", "norm_a", "t", "hT", "b", "sq_b", "ss_b", "sd_b", "rs_b", "norm_b",
                  "scaled", "shifted", "h", "eq", "before", "dup", "mixed", "idx", "counted", "sum", "out", "ones")}
        ea_in = [sem(f"e1_ea_in{i}") for i in range(RING)]
        keys_in = [sem(f"e1_keys_in{i}") for i in range(RING)]
        gathered = [sem(f"e1_gathered{i}") for i in range(RING)]
        added = [sem(f"e1_added{i}") for i in range(K1)]
        issued = sem("e1_issued")
        block = ctx.enter_context(nc.Block())
        at_slot = lambda slot, lag: (slot + lag) % RING

        def sync_steps(sp, windowed):
            for slot, at in quads(sp, 5):
                if (q := at(LOAD)) is not None:
                    if had(q, RING):
                        sp.wait_ge(S["a"], q - 1)
                    sp.dma_start(ea[:, slot].rearrange("p j e -> p (j e)"), k.ea_T[:, bass.ds(q * QE, QE)]).then_inc(ea_in[slot], 16)
                if (q := at(5)) is not None and not windowed:
                    slot = at_slot(slot, 5)
                    if had(q, RING):
                        sp.wait_ge(S["eq"], q - 1)
                    sp.dma_start(keys[:, slot, :], k.dst_row[bass.ds(q * QE, QE)].partition_broadcast(P)).then_inc(keys_in[slot], 16)

        def gpsimd_steps(pool, windowed):
            for slot, at in quads(pool, LAG):
                if (q := at(SHIFT)) is not None:
                    s = at_slot(slot, SHIFT)
                    pool.wait_ge(S["scaled"], q + 1)
                    if had(q, RING):
                        pool.wait_ge(S["h"], q - 1)
                    nc.gpsimd.tensor_tensor(shifted_b[:, s, :], norm_b[:, s, :], k.g1b_b_all[:].rearrange("p j c -> p (j c)"),
                                            ALU.add).then_inc(S["shifted"], 1)
                q, s = at(SCATTER), at_slot(slot, SCATTER)
                if q is not None and windowed and s == RING - 1:
                    w = at(SCATTER, RING)
                    pool.wait_ge(S["out"], w + 1)
                    if had(w, 1):
                        pool.wait_ge(added[0], w * 16)
                    pool.sem_inc(issued, 1)
                    first = pool.value_load(k.base_i[0:1, bass.ds(w, 1)], min_val=0, max_val=N)
                    nc.gpsimd.dma_start(k.sums1[0][bass.ds(first, P), :], window_sums[:], accum_op=ALU.add).then_inc(added[0], 16)
                if q is not None and not windowed:
                    pool.wait_ge(S["out"], q + 1)
                    pool.wait_ge(S["counted"], q + 1)
                    pool.wait_ge(S["idx"], q + 1)
                    for j in range(QT):
                        if had(q, 1) or j >= K1:
                            pool.wait_ge(added[j % K1], q * (16 * QT // K1) + 16 * (j // K1))
                        pool.sem_inc(issued, 1)
                        nc.gpsimd.indirect_dma_start(k.sums1[j % K1], bass.IndirectOffsetOnAxis(ap=idx[:, s, j:j + 1], axis=0),
                                                     merged[:, s, j, :], None, compute_op=ALU.add).then_inc(added[j % K1], 16)
                if (q := at(GATHER)) is not None:
                    s = at_slot(slot, GATHER)
                    pool.wait_ge(S["xa_idx"], q + 1)
                    if had(q, RING):
                        pool.wait_ge(S["a"], q - 1)
                        pool.wait_ge(S["sum_a"], q - 1)
                    pool.sem_inc(issued, 1)
                    for j in range(QT):
                        nc.gpsimd.indirect_dma_start(xa[:, s, j, :], None, k.xa,
                                                     bass.IndirectOffsetOnAxis(ap=xa_idx[:, s, j:j + 1], axis=0)).then_inc(gathered[s], 16)
            if windowed:
                pool.wait_ge(added[0], 16 * W)
            else:
                for table in range(K1):
                    pool.wait_ge(added[table], 16 * QT // K1 * Q)

        def tensor_steps(pe, windowed):
            for slot, at in quads(pe, MERGE):
                if (q := at(B)) is not None:
                    s = at_slot(slot, B)
                    pe.wait_ge(S["hT"], q + 1)
                    if had(q, 1):
                        pe.wait_ge(S["norm_b"], q)
                    nc.tensor.matmul(psB[:].rearrange("p j c -> p (j c)"), k.ones3[:], k.b1b_rows[:].rearrange("i j c -> i (j c)"), start=True, stop=False)
                    for j in range(QT):
                        nc.tensor.matmul(psB[:, j, :], hT[:, s, 0, j, :], k.w1b_c[:, 0, :], start=False, stop=False)
                        last = nc.tensor.matmul(psB[:, j, :], hT[:, s, 1, j, :], k.w1b_c[:, 1, :], start=False, stop=j == QT - 1)
                    last.then_inc(S["b"], 1)
                if (q := at(TURN)) is not None:
                    s = at_slot(slot, TURN)
                    pe.wait_ge(S["norm_a"], q + 1)
                    if had(q, 1):
                        pe.wait_ge(S["hT"], q)
                    for half in range(2):
                        for j in range(QT):
                            last = nc.tensor.transpose(psT[:, half, j, :], norm_a[:, s, j, half * P:(half + 1) * P], k.eye[:])
                    last.then_inc(S["t"], 1)
                if (q := at(A)) is not None:
                    s = at_slot(slot, A)
                    pe.wait_ge(ea_in[s], uses(q, s, 16))
                    if had(q, RING):
                        pe.wait_ge(S["norm_a"], q - 1)
                    pe.wait_ge(gathered[s], uses(q, s, 16 * QT))
                    for j in range(PE_ADDS, QT):
                        last = nc.tensor.matmul(psA[:, s, j, :], ea[:, s, j, :], k.w1a_e[:], start=True, stop=True)
                    last.then_inc(S["a_edge"], 1)
                    for j in range(PE_ADDS):
                        nc.tensor.matmul(psA[:, s, j, :], ea[:, s, j, :], k.w1a_e[:], start=True, stop=False)
                        last = nc.tensor.matmul(psA[:, s, j, :], k.eye[:], xa[:, s, j, :], start=False, stop=True)
                    last.then_inc(S["a"], 1)
                if (q := at(MERGE)) is not None:
                    s = at_slot(slot, MERGE)
                    pe.wait_ge(S["h"], q + 1)
                    if isinstance(q, int) and q == 0:
                        pe.wait_ge(S["ones"], 1)
                    pe.wait_ge(S["eq"], q + 1)
                    if windowed:
                        w = at(MERGE, RING)
                        if s == 0 and had(w, 1):
                            pe.wait_ge(S["out"], w)
                        for j in range(QT):
                            last = nc.tensor.matmul(psM[:, 0:SW], eq[:, s, j, :], h[:, s, j, :], start=s == 0 and j == 0,
                                                    stop=s == RING - 1 and j == QT - 1)
                    else:
                        if had(q, 1):
                            pe.wait_ge(S["out"], q)
                        for j in range(QT):
                            last = nc.tensor.matmul(psM[:, j * C:(j + 1) * C], eq[:, s, j, :], h[:, s, j, 0:C], start=True, stop=True)
                    last.then_inc(S["sum"], 1)

        def scalar_steps(act, windowed):
            flat = lambda x: x.rearrange("p j c -> p (j c)")
            for slot, at in quads(act, MERGE):
                if (q := at(GN_A)) is not None:
                    s = at_slot(slot, GN_A)
                    act.wait_ge(S["ss_a"], q + 1)
                    if had(q, RING):
                        act.wait_ge(S["rs_a"], q - 1)
                    nc.scalar.activation(sd_a[:, s, :], ss_a[:, s, :], ACT.Sqrt, bias=k.eps[:], scale=float(G) / H).then_inc(S["sd_a"], 1)
                if (q := at(GN_B)) is not None:
                    s = at_slot(slot, GN_B)
                    act.wait_ge(S["b"], q + 1)
                    if had(q, RING):
                        act.wait_ge(S["ss_b"], q - 1)
                    nc.scalar.activation(sq_b[:, s, :], flat(psB[:]), ACT.Square).then_inc(S["sq_b"], 1)
                if (q := at(TURN)) is not None:
                    s = at_slot(slot, TURN)
                    act.wait_ge(S["t"], q + 1)
                    if had(q, RING):
                        act.wait_ge(S["b"], q - 1)
                    for half in range(2):
                        last = nc.scalar.activation(flat(hT[:, s, half]), flat(psT[:, half]), ACT.Relu,
                                                    bias=k.gn1a[:, 1, half:half + 1], scale=k.gn1a[:, 0, half:half + 1])
                    last.then_inc(S["hT"], 1)
                if (q := at(GN_B)) is not None:
                    s = at_slot(slot, GN_B)
                    act.wait_ge(S["ss_b"], q + 1)
                    if had(q, RING):
                        act.wait_ge(S["rs_b"], q - 1)
                    nc.scalar.activation(sd_b[:, s, :], ss_b[:, s, :], ACT.Sqrt, bias=k.eps[:], scale=float(G) / C).then_inc(S["sd_b"], 1)
                if (q := at(RELU_B)) is not None:
                    s = at_slot(slot, RELU_B)
                    act.wait_ge(S["shifted"], q + 1)
                    if had(q, RING):
                        act.wait_ge(S["sum"], q - 1)
                    nc.scalar.activation(h[:, s, :, 0:C], shifted_b[:, s, :].rearrange("p (j c) -> p j c", j=QT), ACT.Relu).then_inc(S["h"], 1)
                if (q := at(ADD)) is not None:
                    s = at_slot(slot, ADD)
                    act.wait_ge(S["a"], q + 1)
                    act.wait_ge(S["sum_a"], q + 1)
                    if had(q, RING):
                        act.wait_ge(S["ss_a"], q - 1)
                    nc.scalar.activation(sq_a[:, s, :], flat(psA[:, s]), ACT.Square).then_inc(S["sq_a"], 1)
                q, s = at(MERGE), at_slot(slot, MERGE)
                if q is not None and windowed and s == RING - 1:
                    w = at(MERGE, RING)
                    act.wait_ge(S["sum"], q + 1)
                    if had(w, 1):
                        act.wait_ge(added[0], w * 16)
                    nc.scalar.copy(window_sums[:], psM[:, 0:SW]).then_inc(S["out"], 1)
                if q is not None and not windowed:
                    act.wait_ge(S["sum"], q + 1)
                    if had(q, RING):
                        for table in range(K1):
                            act.wait_ge(added[table], q * (16 * QT // K1) - 16 * QT // K1)
                    nc.scalar.copy(merged[:, s, :, 0:C], psM[:].rearrange("p (j c) -> p j c", j=QT)).then_inc(S["out"], 1)

        def vector_steps(dve, windowed):
            groups = lambda x, n: x.rearrange("p (g k) -> p g k", g=n)
            nc.vector.memset(h[:, :, :, C:SW], 1.0).then_inc(S["ones"], 1)
            for slot, at in quads(dve, EQ):
                if (q := at(GN_A)) is not None:
                    s = at_slot(slot, GN_A)
                    dve.wait_ge(S["sq_a"], q + 1)
                    if had(q, RING):
                        dve.wait_ge(S["sd_a"], q - 1)
                    nc.vector.tensor_reduce(ss_a[:, s, :], groups(sq_a[:, s, :], QT * G), AX.X, ALU.add).then_inc(S["ss_a"], 1)
                if (q := at(SCALE)) is not None:
                    s = at_slot(slot, SCALE)
                    dve.wait_ge(S["norm_b"], q + 1)
                    nc.vector.tensor_tensor(norm_b[:, s, :], norm_b[:, s, :], k.g1b_w_all[:].rearrange("p j c -> p (j c)"),
                                            ALU.mult).then_inc(S["scaled"], 1)
                if (q := at(LOAD)) is not None:
                    if had(q, RING):
                        dve.wait_ge(gathered[slot], uses(q - RING, slot, 16 * QT))
                    nc.vector.tensor_copy(xa_idx[:, slot, :], k.src_idx[:, bass.ds(q * QT, QT)]).then_inc(S["xa_idx"], 1)
                if (q := at(GN_A)) is not None:
                    s = at_slot(slot, GN_A)
                    dve.wait_ge(S["sd_a"], q + 1)
                    nc.vector.reciprocal(rs_a[:, s, :], sd_a[:, s, :]).then_inc(S["rs_a"], 1)
                    dve.wait_ge(S["rs_a"], q + 1)
                    if had(q, RING):
                        dve.wait_ge(S["t"], q - 1)
                    nc.vector.tensor_tensor(norm_a[:, s].rearrange("p j (g k) -> p (j g) k", g=G), psA[:, s].rearrange("p j (g k) -> p (j g) k", g=G),
                                            spread(rs_a[:, s, :], P, H // G), ALU.mult).then_inc(S["norm_a"], 1)
                if (q := at(EQ)) is not None:
                    s = at_slot(slot, EQ)
                    if had(q, RING):
                        dve.wait_ge(S["sum"], q - 1)
                    if windowed:
                        nc.vector.tensor_tensor(eq[:, s], k.iota[:].unsqueeze(1).broadcast_to((P, QT, P)), spread(k.rel[:, bass.ds(q * QT, QT)], P, P),
                                                ALU.is_equal).then_inc(S["eq"], 1)
                    else:
                        dve.wait_ge(keys_in[s], uses(q, s, 16))
                        compare_keys(nc, keys[:, s, :], k.dst_f, q, eq[:, s], S["eq"])
                        dve.wait_ge(S["eq"], q + 1)
                        if had(q, RING):
                            for table in range(K1):
                                dve.wait_ge(added[table], q * (16 * QT // K1) - 16 * QT // K1)
                        nc.vector.tensor_reduce(merged[:, s, :, C:SW], eq[:, s], AX.X, ALU.add).then_inc(S["counted"], 1)
                        first_of_key(nc, dve, q, k.lower[:], eq[:, s], before[:], k.dst_f, k.dst_trash, dup[:], mixed[:],
                                     idx[:, s, :], S["before"], S["dup"], S["mixed"], S["idx"])
                if (q := at(GN_B)) is not None:
                    s = at_slot(slot, GN_B)
                    dve.wait_ge(S["sq_b"], q + 1)
                    if had(q, RING):
                        dve.wait_ge(S["sd_b"], q - 1)
                    nc.vector.tensor_reduce(ss_b[:, s, :], groups(sq_b[:, s, :], QT * G), AX.X, ALU.add).then_inc(S["ss_b"], 1)
                if (q := at(ADD)) is not None:
                    s = at_slot(slot, ADD)
                    dve.wait_ge(S["a_edge"], q + 1)
                    dve.wait_ge(gathered[s], uses(q, s, 16 * QT))
                    nc.vector.tensor_tensor(psA[:, s, PE_ADDS:QT], psA[:, s, PE_ADDS:QT], xa[:, s, PE_ADDS:QT], ALU.add).then_inc(S["sum_a"], 1)
                if (q := at(GN_B)) is not None:
                    s = at_slot(slot, GN_B)
                    dve.wait_ge(S["sd_b"], q + 1)
                    nc.vector.reciprocal(rs_b[:, s, :], sd_b[:, s, :]).then_inc(S["rs_b"], 1)
                    dve.wait_ge(S["rs_b"], q + 1)
                    if had(q, RING):
                        dve.wait_ge(S["shifted"], q - 1)
                    nc.vector.tensor_tensor(groups(norm_b[:, s, :], QT * G), psB[:].rearrange("p j (g k) -> p (j g) k", g=G),
                                            spread(rs_b[:, s, :], P, C // G), ALU.mult).then_inc(S["norm_b"], 1)

        @block.sync
        def _(sp):
            either(k, sp, sync_steps)

        @block.gpsimd
        def _(pool):
            either(k, pool, gpsimd_steps)

        @block.tensor
        def _(pe):
            either(k, pe, tensor_steps)

        @block.scalar
        def _(act):
            either(k, act, scalar_steps)

        @block.vector
        def _(dve):
            either(k, dve, vector_steps)


def phase_nodes2(nc, k):
    LOAD, MEAN, HIDDEN, OUT, LAST, STORE = 0, 1, 2, 3, 4, 5
    with ExitStack() as ctx:
        sb = lambda n, s, d: ctx.enter_context(nc.sbuf_tensor(n, s, d))
        sem = lambda n: ctx.enter_context(nc.semaphore(n))
        sums = sb("n2_sums", [P, RING, K1, NB, SW], FP32)
        x1 = sb("n2_x1", [P, RING, NB, C], FP32)
        xT = sb("n2_xT", [P, RING, NB, P], FP32)
        total = sb("n2_total", [P, NB, SW], FP32)
        agg = sb("n2_agg", [P, NB, C], FP32)
        aggT = sb("n2_aggT", [P, NB, P], FP32)
        sq = sb("n2_sq", [P, NB, H], FP32)
        norm = sb("n2_norm", [P, NB, H], FP32)
        hT = sb("n2_hT", [P, 2, NB, P], FP32)
        z = sb("n2_z", [P, NB, C], FP32)
        sq2 = sb("n2_sq2", [P, NB, C], FP32)
        out = sb("n2_out", [P, RING, NB, C], FP32)
        cnt, mean, ss2, sd2, rs2 = (sb(f"n2_{n}", [P, NB], FP32) for n in ("cnt", "mean", "ss2", "sd2", "rs2"))
        ss, sd, rs = (sb(f"n2_{n}", [P, NB * G], FP32) for n in ("ss", "sd", "rs"))
        psT = ctx.enter_context(nc.psum_tensor("n2_psT", [P, 8, P], FP32))
        psZ = ctx.enter_context(nc.psum_tensor("n2_psZ", [P, 8, P], FP32))
        psU = ctx.enter_context(nc.psum_tensor("n2_psU", [P, 8, H], FP32))
        psH = psU[:].rearrange("p a (b n) -> p (a b) n", b=2)
        S = {n: sem(f"n2_{n}_ready") for n in ("count", "agg", "t", "aggT", "u", "sq", "ss", "sd", "rs", "norm", "th", "hT", "z",
                                               "mean", "centred", "sq2", "ss2", "sd2", "rs2", "out")}
        loaded = [sem(f"n2_loaded{i}") for i in range(RING)]
        x1_in = [sem(f"n2_x1_in{i}") for i in range(RING)]
        stored = [sem(f"n2_stored{i}") for i in range(RING)]
        block = ctx.enter_context(nc.Block())
        at_slot = lambda slot, lag: (slot + lag) % RING

        @block.sync
        def _(sp):
            for slot, at in pipeline(sp, BLOCKS, STORE):
                if (b := at(LOAD)) is not None:
                    if had(b, RING):
                        sp.wait_ge(S["agg"], b - 1)
                        sp.wait_ge(S["u"], b - 1)
                    for c in range(K1):
                        sp.dma_start(sums[:, slot, c], node_rows(k.sums1[c], b)).then_inc(loaded[slot], 16)
                    sp.dma_start(xT[:, slot].rearrange("p j n -> p (j n)"), k.x1T[bass.ds(b, 1)].rearrange("a p m -> (a p) m")).then_inc(loaded[slot], 16)
                if (b := at(HIDDEN)) is not None:
                    s = at_slot(slot, HIDDEN)
                    if had(b, RING):
                        sp.wait_ge(S["centred"], b - 1)
                    sp.dma_start(x1[:, s], node_rows(k.x1, b)).then_inc(x1_in[s], 16)
                if (b := at(STORE)) is not None:
                    s = at_slot(slot, STORE)
                    sp.wait_ge(S["out"], b + 1)
                    sp.dma_start(node_rows(k.out, b), out[:, s]).then_inc(stored[s], 16)
            for slot in range(RING):
                sp.wait_ge(stored[slot], 16 * (BLOCKS // RING))

        @block.vector
        def _(dve):
            for slot, at in pipeline(dve, BLOCKS, LAST):
                if (b := at(LAST)) is not None:
                    s = at_slot(slot, LAST)
                    dve.wait_ge(S["z"], b + 1)
                    dve.wait_ge(x1_in[s], uses(b, s, 16))
                    if had(b, 1):
                        dve.wait_ge(S["out"], b)
                    chain = Chain(dve, S["mean"], 3, b)
                    chain.then(nc.vector.tensor_tensor(z[:], psZ[:, 0:NB, :], x1[:, s], ALU.add))
                    chain.then(nc.vector.tensor_reduce(mean[:], z[:], AX.X, ALU.add))
                    chain.then(nc.vector.tensor_scalar(mean[:], mean[:], 1.0 / C, None, ALU.mult))
                    nc.vector.tensor_tensor(z[:], z[:], spread(mean[:], P, C), ALU.subtract).then_inc(S["centred"], 1)
                if (b := at(MEAN)) is not None:
                    s = at_slot(slot, MEAN)
                    dve.wait_ge(loaded[s], uses(b, s, 16 * (K1 + 1)))
                    if had(b, 1):
                        dve.wait_ge(S["agg"], b)
                    chain = Chain(dve, S["count"], K1 - 1 + 2, b)
                    chain.then(nc.vector.tensor_tensor(total[:], sums[:, s, 0], sums[:, s, 1], ALU.add))
                    for c in range(2, K1):
                        chain.then(nc.vector.tensor_tensor(total[:], total[:], sums[:, s, c], ALU.add))
                    chain.then(nc.vector.tensor_scalar(cnt[:], total[:, :, C], 1.0, None, ALU.max))
                    chain.then(nc.vector.reciprocal(cnt[:], cnt[:]))
                    if had(b, 1):
                        dve.wait_ge(S["t"], b)
                    nc.vector.tensor_tensor(agg[:], total[:, :, 0:C], spread(cnt[:], P, C), ALU.mult).then_inc(S["agg"], 1)
                if (b := at(LAST)) is not None:
                    s = at_slot(slot, LAST)
                    dve.wait_ge(S["sq2"], b + 1)
                    nc.vector.tensor_reduce(ss2[:], sq2[:], AX.X, ALU.add).then_inc(S["ss2"], 1)
                    dve.wait_ge(S["sd2"], b + 1)
                    nc.vector.reciprocal(rs2[:], sd2[:]).then_inc(S["rs2"], 1)
                    dve.wait_ge(S["rs2"], b + 1)
                    if had(b, RING):
                        dve.wait_ge(stored[s], uses(b - RING, s, 16))
                    nc.vector.tensor_tensor(out[:, s], z[:], spread(rs2[:], P, C), ALU.mult).then_inc(S["out"], 1)
                if (b := at(HIDDEN)) is not None:
                    dve.wait_ge(S["sq"], b + 1)
                    nc.vector.tensor_reduce(ss[:], sq[:].rearrange("p j (g k) -> p (j g) k", g=G), AX.X, ALU.add).then_inc(S["ss"], 1)
                    dve.wait_ge(S["sd"], b + 1)
                    nc.vector.reciprocal(rs[:], sd[:]).then_inc(S["rs"], 1)
                    dve.wait_ge(S["rs"], b + 1)
                    if had(b, 1):
                        dve.wait_ge(S["th"], b)
                    nc.vector.tensor_tensor(norm[:].rearrange("p j (g k) -> p (j g) k", g=G), psU[:, 0:NB, :].rearrange("p j (g k) -> p (j g) k", g=G),
                                            spread(rs[:], P, H // G), ALU.mult).then_inc(S["norm"], 1)

        @block.scalar
        def _(act):
            for slot, at in pipeline(act, BLOCKS, LAST):
                if (b := at(LAST)) is not None:
                    act.wait_ge(S["centred"], b + 1)
                    nc.scalar.activation(sq2[:], z[:], ACT.Square).then_inc(S["sq2"], 1)
                    act.wait_ge(S["ss2"], b + 1)
                    nc.scalar.activation(sd2[:], ss2[:], ACT.Sqrt, bias=k.eps[:], scale=1.0 / C).then_inc(S["sd2"], 1)
                if (b := at(HIDDEN)) is not None:
                    act.wait_ge(S["u"], b + 1)
                    nc.scalar.activation(sq[:], psU[:, 0:NB, :], ACT.Square).then_inc(S["sq"], 1)
                if (b := at(MEAN)) is not None:
                    act.wait_ge(S["t"], b + 1)
                    if had(b, 1):
                        act.wait_ge(S["u"], b)
                    nc.scalar.copy(aggT[:], psT[:, 0:NB, :]).then_inc(S["aggT"], 1)
                if (b := at(HIDDEN)) is not None:
                    act.wait_ge(S["ss"], b + 1)
                    nc.scalar.activation(sd[:], ss[:], ACT.Sqrt, bias=k.eps[:], scale=float(G) / H).then_inc(S["sd"], 1)
                    act.wait_ge(S["th"], b + 1)
                    if had(b, 1):
                        act.wait_ge(S["z"], b)
                    for half in range(2):
                        last = nc.scalar.activation(hT[:, half], psH[:, half * 8:half * 8 + NB, :], ACT.Relu,
                                                    bias=k.gn2a[:, 1, half:half + 1], scale=k.gn2a[:, 0, half:half + 1])
                    last.then_inc(S["hT"], 1)

        @block.tensor
        def _(pe):
            for slot, at in pipeline(pe, BLOCKS, OUT):
                if (b := at(HIDDEN)) is not None:
                    s = at_slot(slot, HIDDEN)
                    pe.wait_ge(loaded[s], uses(b, s, 16 * (K1 + 1)))
                    pe.wait_ge(S["aggT"], b + 1)
                    if had(b, 1):
                        pe.wait_ge(S["hT"], b)
                    for j in range(NB):
                        nc.tensor.matmul(psU[:, j, :], k.ones3[:], k.b2a_row[:], start=True, stop=False)
                        nc.tensor.matmul(psU[:, j, :], xT[:, s, j, :], k.w2a_x[:], start=False, stop=False)
                        last = nc.tensor.matmul(psU[:, j, :], aggT[:, j, :], k.w2a_g[:], start=False, stop=True)
                    last.then_inc(S["u"], 1)
                if (b := at(MEAN)) is not None:
                    pe.wait_ge(S["agg"], b + 1)
                    if had(b, 1):
                        pe.wait_ge(S["aggT"], b)
                    for j in range(NB):
                        last = nc.tensor.transpose(psT[:, j, :], agg[:, j, :], k.eye[:])
                    last.then_inc(S["t"], 1)
                if (b := at(OUT)) is not None:
                    pe.wait_ge(S["hT"], b + 1)
                    if had(b, 1):
                        pe.wait_ge(S["centred"], b)
                    for j in range(NB):
                        nc.tensor.matmul(psZ[:, j, :], k.ones3[:], k.b2b_row[:], start=True, stop=False)
                        nc.tensor.matmul(psZ[:, j, :], hT[:, 0, j, :], k.w2b_c[:, 0, :], start=False, stop=False)
                        last = nc.tensor.matmul(psZ[:, j, :], hT[:, 1, j, :], k.w2b_c[:, 1, :], start=False, stop=True)
                    last.then_inc(S["z"], 1)
                if (b := at(HIDDEN)) is not None:
                    pe.wait_ge(S["norm"], b + 1)
                    for half in range(2):
                        for j in range(NB):
                            last = nc.tensor.transpose(psH[:, half * 8 + j, :], norm[:, j, half * P:(half + 1) * P], k.eye[:])
                    last.then_inc(S["th"], 1)


def build(nc, k):
    k.y = nc.dram_tensor("y_table", (ROWS, R * C), FP32, kind="Internal").ap()
    k.sums0 = [nc.dram_tensor(f"sums0_{c}", (ROWS, C), FP32, kind="Internal").ap() for c in range(K0)]
    k.sums1 = [nc.dram_tensor(f"sums1_{c}", (ROWS, SW), FP32, kind="Internal").ap() for c in range(K1)]
    k.xa = nc.dram_tensor("xa_table", (N, H), FP32, kind="Internal").ap()
    k.x1 = nc.dram_tensor("x1_table", (N, C), FP32, kind="Internal").ap()
    k.x1T = nc.dram_tensor("x1T_blocks", (BLOCKS, P, BN), FP32, kind="Internal").ap()
    with ExitStack() as ctx:
        sb = lambda n, s, d: ctx.enter_context(nc.sbuf_tensor(n, s, d))
        k.src_idx = sb("src_idx", [P, T], I32)
        k.type_i = sb("type_i", [P, T], I32)
        k.src_f = sb("src_f", [P, T], FP32)
        k.dst_f = sb("dst_f", [P, T], FP32)
        k.src_trash = sb("src_trash", [P, T], FP32)
        k.dst_trash = sb("dst_trash", [P, T], FP32)
        k.zeros = sb("zeros", [P, ZEROS], FP32)
        k.rel = sb("rel", [P, T], FP32)
        k.base_y = sb("base_y", [P, W], FP32)
        k.iota_y = sb("iota_y", [P, R], FP32)
        k.base_i = sb("base_i", [1, W], I32)
        k.windowed = sb("windowed", [1, 1], I32)
        k.iota = sb("iota", [P, P], FP32)
        k.lower = sb("lower", [P, P], FP32)
        k.eye = sb("eye", [P, P], FP32)
        k.eps = sb("eps", [P, 1], FP32)
        k.ones3 = sb("ones3", [3, P], BF16)
        k.w1a_x, k.w1a_e, k.w2a_x, k.w2a_g, k.b1a_all = (sb(n, [P, H], FP32) for n in ("w1a_x", "w1a_e", "w2a_x", "w2a_g", "b1a_all"))
        k.w1b_c, k.w2b_c = sb("w1b_c", [P, 2, C], FP32), sb("w2b_c", [P, 2, C], FP32)
        k.gn1a, k.gn2a = sb("gn1a", [P, 2, 2], FP32), sb("gn2a", [P, 2, 2], FP32)
        k.g1b_w_all, k.g1b_b_all = sb("g1b_w_all", [P, QT, C], FP32), sb("g1b_b_all", [P, QT, C], FP32)
        k.bias0_all = sb("bias0_all", [P, C], FP32)
        k.b1b_rows, k.b2a_row, k.b2b_row = sb("b1b_rows", [3, QT, C], BF16), sb("b2a_row", [3, H], BF16), sb("b2b_row", [3, C], BF16)
        phase_tables(nc, k)
        phase_weights(nc, k)
        phase_edges0(nc, k)
        phase_nodes1(nc, k)
        phase_edges1(nc, k)
        phase_nodes2(nc, k)


def padded(a, rows, fill):
    return np.concatenate([a, np.full((rows - a.shape[0],) + a.shape[1:], fill, a.dtype)])


def kernel(**inputs):
    import concourse.bacc as bacc
    from concourse.bass_utils import run_bass_kernel_spmd

    a = {n: np.asarray(v) for n, v in inputs.items()}
    src, dst = (padded(a[n].astype(np.int32, copy=False), T * P, NODES) for n in ("src", "dst"))
    types = padded(a["edge_type_8"].astype(np.int32, copy=False), T * P, 0)
    x = padded(a["x"], N, 0)
    columns = lambda v: np.ascontiguousarray(v.reshape(T, P).T)
    arrays = {
        "x": x, "x_T": np.ascontiguousarray(x.T), "src_row": src, "dst_row": dst,
        "base_row": np.ascontiguousarray(dst[::WINDOW]), "src_cols": columns(src), "dst_cols": columns(dst), "type_cols": columns(types), "type_row": types,
        "ea_T": np.ascontiguousarray(padded(a["edge_attr_128"], T * P, 0).T),
        "w_rel": np.ascontiguousarray(a["L0_gnn_weight"].transpose(1, 0, 2).reshape(C, R * C)),
        "bias0": a["L0_gnn_bias"], "W1a": a["L1_gnn_W1a"], "b1a": a["L1_gnn_b1a"], "W1b": a["L1_gnn_W1b"], "b1b": a["L1_gnn_b1b"],
        "W2a": a["L1_gnn_W2a"], "b2a": a["L1_gnn_b2a"], "W2b": a["L1_gnn_W2b"], "b2b": a["L1_gnn_b2b"],
        "g1a_w": a["L1_gnn_gn1a_w"], "g1a_b": a["L1_gnn_gn1a_b"], "g1b_w": a["L1_gnn_gn1b_w"], "g1b_b": a["L1_gnn_gn1b_b"],
        "g2a_w": a["L1_gnn_gn2a_w"], "g2a_b": a["L1_gnn_gn2a_b"],
    }
    nc = bacc.Bacc("TRN2", target_bir_lowering=False, num_devices=1)
    aps = {n: nc.dram_tensor(f"in_{n}", v.shape, mybir.dt.from_np(v.dtype), kind="ExternalInput").ap() for n, v in arrays.items()}
    k = Names()
    k.x, k.x_T, k.src_row, k.dst_row = (aps[n] for n in ("x", "x_T", "src_row", "dst_row"))
    k.src_cols, k.dst_cols, k.type_cols, k.ea_T = (aps[n] for n in ("src_cols", "dst_cols", "type_cols", "ea_T"))
    k.base_row, k.type_row = aps["base_row"], aps["type_row"]
    k.w_rel, k.bias0 = aps["w_rel"], aps["bias0"]
    k.W1a, k.b1a, k.W1b, k.b1b = (aps[n] for n in ("W1a", "b1a", "W1b", "b1b"))
    k.W2a, k.b2a, k.W2b, k.b2b = (aps[n] for n in ("W2a", "b2a", "W2b", "b2b"))
    k.g1a_w, k.g1a_b, k.g1b_w, k.g1b_b, k.g2a_w, k.g2a_b = (aps[n] for n in ("g1a_w", "g1a_b", "g1b_w", "g1b_b", "g2a_w", "g2a_b"))
    k.out = nc.dram_tensor("out", (N, C), FP32, kind="ExternalOutput").ap()
    build(nc, k)
    r = run_bass_kernel_spmd(nc, [{f"in_{n}": v for n, v in arrays.items()}], core_ids=[0])
    return r.results[0]["out"][0:NODES]
```
